# Optimizing a Trainium2 kernel written in Bass

```python
import numpy as np
import jax
import jax.numpy as jnp

def _softmax(x, axis=-1):
    return jax.nn.softmax(x, axis=axis)

def _gelu(x):
    return jax.nn.gelu(x, approximate=True)

def _silu(x):
    return jax.nn.silu(x)

def _sigmoid(x):
    return jax.nn.sigmoid(x)

def _layernorm(x, axis=-1, eps=1e-05):
    m = jnp.mean(x, axis=axis, keepdims=True)
    v = jnp.var(x, axis=axis, keepdims=True)
    return (x - m) / jnp.sqrt(v + eps)

def _scatter_add(tgt, idx, src, axis=0):
    return tgt.at[idx].add(src)

def _segment_sum(src, seg, n):
    return jax.ops.segment_sum(src, seg, n)
kernel_name = 'mk_xattn_seq_d2_seqx_r4_9ce29e'

def setup_inputs(seed: int=0):
    np.random.seed(seed)
    _w = jnp.asarray

    def _rec_inputs():
        import jax
        import jax.numpy as jnp
        _rk = jax.random.key(seed)
        x = -0.0002928 + 1 * jax.random.normal(jax.random.fold_in(_rk, 1), (32, 112, 256), jnp.float32)
        _lenS = 112 - jax.random.randint(jax.random.fold_in(_rk, 7), (32,), 0, max(1, 112 // 4) + 1, jnp.int32)
        _lenS2 = 375 - jax.random.randint(jax.random.fold_in(_rk, 8), (32,), 0, max(1, 375 // 4) + 1, jnp.int32)
        _ctx_1024P = jax.random.normal(jax.random.fold_in(_rk, 11), (32, 16, 256), jnp.float32)
        _ctx_1024c = jax.random.dirichlet(jax.random.fold_in(_rk, 511), 0.3 * jnp.ones((16,), jnp.float32), (32, 375))
        _ctx_1024t = jnp.einsum('bsk,bkd->bsd', _ctx_1024c, _ctx_1024P)
        _ctx_1024t = _ctx_1024t * jax.lax.rsqrt(jnp.mean(jnp.square(_ctx_1024t)) + 1e-12) * 0.953939
        ctx_1024 = 4.13588e-05 + 0.999923 * (_ctx_1024t + 0.3 * jax.random.normal(jax.random.fold_in(_rk, 611), (32, 375, 256), jnp.float32))
        return (x, ctx_1024)
    x, ctx_1024 = _rec_inputs()

    def _L0_xattn_setup():
        import jax, jax.numpy as jnp
        import numpy as np
        D_MODEL = 256
        NUM_HEADS = 16
        HEAD_DIM = D_MODEL // NUM_HEADS
        SCALE = HEAD_DIM ** (-0.5)
        LN_EPS = 1e-05
        Q_EPS = 1e-05

        def bit_quant(W):
            gamma = jnp.mean(jnp.abs(W))
            Wq = jnp.clip(jnp.round(W / (gamma + Q_EPS)), -1.0, 1.0) * gamma
            return W + jax.lax.stop_gradient(Wq - W)

        def layer_norm(x, gamma, beta):
            mu = jnp.mean(x, axis=-1, keepdims=True)
            var = jnp.mean(jnp.square(x - mu), axis=-1, keepdims=True)
            return (x - mu) * jax.lax.rsqrt(var + LN_EPS) * gamma + beta
        key = jax.random.key(seed)
        ks = jax.random.split(key, 8)
        B, T, T_ctx, C = (4, 256, 512, D_MODEL)
        w_std = C ** (-0.5)
        return {'x': jax.random.normal(ks[0], (B, T, C), jnp.float32), 'context': jax.random.normal(ks[1], (B, T_ctx, C), jnp.float32), 'Wq': jax.random.normal(ks[2], (C, C), jnp.float32) * w_std, 'bq': jnp.zeros((C,), jnp.float32), 'Wk': jax.random.normal(ks[3], (C, C), jnp.float32) * w_std, 'bk': jnp.zeros((C,), jnp.float32), 'Wv': jax.random.normal(ks[4], (C, C), jnp.float32) * w_std, 'bv': jnp.zeros((C,), jnp.float32), 'Wo': jax.random.normal(ks[5], (C, C), jnp.float32) * w_std, 'bo': jnp.zeros((C,), jnp.float32), 'ln_gamma': jnp.ones((C,), jnp.float32), 'ln_beta': jnp.zeros((C,), jnp.float32)}
    _L0_xattn_all = _L0_xattn_setup()
    _L0_xattn_in = {k: v for k, v in _L0_xattn_all.items() if k in ('Wq', 'bq', 'Wk', 'bk', 'Wv', 'bv', 'Wo', 'bo', 'ln_gamma', 'ln_beta')}
    del _L0_xattn_all

    def _L1_xattn_setup():
        import jax, jax.numpy as jnp
        import numpy as np
        B, Q, KV = (2, 512, 512)
        D_MODEL = 256
        N_HEADS = 16
        D_KV = 64
        EPS = 1e-06
        key = jax.random.key(seed)
        ks = jax.random.split(key, 7)
        s = 0.02
        return {'hidden_states': jax.random.normal(ks[0], (B, Q, D_MODEL), jnp.float32), 'key_value_states': jax.random.normal(ks[1], (B, KV, D_MODEL), jnp.float32), 'wq': jax.random.normal(ks[2], (D_MODEL, N_HEADS * D_KV), jnp.float32) * s, 'wk': jax.random.normal(ks[3], (D_MODEL, N_HEADS * D_KV), jnp.float32) * s, 'wv': jax.random.normal(ks[4], (D_MODEL, N_HEADS * D_KV), jnp.float32) * s, 'wo': jax.random.normal(ks[5], (N_HEADS * D_KV, D_MODEL), jnp.float32) * s, 'norm_w': jnp.ones((D_MODEL,), jnp.float32)}
    _L1_xattn_all = _L1_xattn_setup()
    _L1_xattn_in = {k: v for k, v in _L1_xattn_all.items() if k in ('wq', 'wk', 'wv', 'wo', 'norm_w')}
    del _L1_xattn_all
    return {'x': x, 'ctx_1024': ctx_1024, 'L0_xattn_Wq': _L0_xattn_in['Wq'], 'L0_xattn_bq': _L0_xattn_in['bq'], 'L0_xattn_Wk': _L0_xattn_in['Wk'], 'L0_xattn_bk': _L0_xattn_in['bk'], 'L0_xattn_Wv': _L0_xattn_in['Wv'], 'L0_xattn_bv': _L0_xattn_in['bv'], 'L0_xattn_Wo': _L0_xattn_in['Wo'], 'L0_xattn_bo': _L0_xattn_in['bo'], 'L0_xattn_ln_gamma': _L0_xattn_in['ln_gamma'], 'L0_xattn_ln_beta': _L0_xattn_in['ln_beta'], 'L1_xattn_wq': _L1_xattn_in['wq'], 'L1_xattn_wk': _L1_xattn_in['wk'], 'L1_xattn_wv': _L1_xattn_in['wv'], 'L1_xattn_wo': _L1_xattn_in['wo'], 'L1_xattn_norm_w': _L1_xattn_in['norm_w']}

def reference(x, ctx_1024, L0_xattn_Wq, L0_xattn_bq, L0_xattn_Wk, L0_xattn_bk, L0_xattn_Wv, L0_xattn_bv, L0_xattn_Wo, L0_xattn_bo, L0_xattn_ln_gamma, L0_xattn_ln_beta, L1_xattn_wq, L1_xattn_wk, L1_xattn_wv, L1_xattn_wo, L1_xattn_norm_w):
    import jax
    import jax.numpy as jnp

    def _L0_xattn_ref(x, context, Wq, bq, Wk, bk, Wv, bv, Wo, bo, ln_gamma, ln_beta):
        import jax, jax.numpy as jnp
        import numpy as np
        D_MODEL = 256
        NUM_HEADS = 16
        HEAD_DIM = D_MODEL // NUM_HEADS
        SCALE = HEAD_DIM ** (-0.5)
        LN_EPS = 1e-05
        Q_EPS = 1e-05

        def bit_quant(W):
            gamma = jnp.mean(jnp.abs(W))
            Wq = jnp.clip(jnp.round(W / (gamma + Q_EPS)), -1.0, 1.0) * gamma
            return W + jax.lax.stop_gradient(Wq - W)

        def layer_norm(x, gamma, beta):
            mu = jnp.mean(x, axis=-1, keepdims=True)
            var = jnp.mean(jnp.square(x - mu), axis=-1, keepdims=True)
            return (x - mu) * jax.lax.rsqrt(var + LN_EPS) * gamma + beta
        B, T, C = x.shape
        T_ctx = context.shape[1]
        residual = x
        xn = layer_norm(x, ln_gamma, ln_beta)
        q = xn @ bit_quant(Wq).T + bq
        k = context @ bit_quant(Wk).T + bk
        v = context @ bit_quant(Wv).T + bv
        q = q.reshape(B, T, NUM_HEADS, HEAD_DIM)
        k = k.reshape(B, T_ctx, NUM_HEADS, HEAD_DIM)
        v = v.reshape(B, T_ctx, NUM_HEADS, HEAD_DIM)
        scores = jnp.einsum('bqhd,bkhd->bhqk', q, k) * SCALE
        probs = jax.nn.softmax(scores, axis=-1)
        out = jnp.einsum('bhqk,bkhd->bqhd', probs, v).reshape(B, T, C)
        return residual + (out @ bit_quant(Wo).T + bo)

    def _L1_xattn_ref(hidden_states, key_value_states, wq, wk, wv, wo, norm_w):
        import jax, jax.numpy as jnp
        import numpy as np
        B, Q, KV = (2, 512, 512)
        D_MODEL = 256
        N_HEADS = 16
        D_KV = 64
        EPS = 1e-06
        var = jnp.mean(jnp.square(hidden_states), axis=-1, keepdims=True)
        normed = hidden_states * jax.lax.rsqrt(var + EPS) * norm_w
        b, q_len, _ = hidden_states.shape
        kv_len = key_value_states.shape[1]

        def split_heads(x):
            return x.reshape(b, -1, N_HEADS, D_KV).transpose(0, 2, 1, 3)
        q = split_heads(normed @ wq)
        k = split_heads(key_value_states @ wk)
        v = split_heads(key_value_states @ wv)
        scores = jnp.einsum('bhqd,bhkd->bhqk', q, k)
        attn = jax.nn.softmax(scores.astype(jnp.float32), axis=-1).astype(scores.dtype)
        ctx = jnp.einsum('bhqk,bhkd->bhqd', attn, v)
        ctx = ctx.transpose(0, 2, 1, 3).reshape(b, q_len, N_HEADS * D_KV)
        attn_out = ctx @ wo
        return hidden_states + attn_out
    x = _L0_xattn_ref(x, ctx_1024, L0_xattn_Wq, L0_xattn_bq, L0_xattn_Wk, L0_xattn_bk, L0_xattn_Wv, L0_xattn_bv, L0_xattn_Wo, L0_xattn_bo, L0_xattn_ln_gamma, L0_xattn_ln_beta)
    x = _L1_xattn_ref(x, ctx_1024, L1_xattn_wq, L1_xattn_wk, L1_xattn_wv, L1_xattn_wo, L1_xattn_norm_w)
    return x

_drawn_inputs = setup_inputs


def setup_inputs(seed=0):
    import zlib

    import numpy as np

    out = dict(_drawn_inputs(seed))
    spreads = {'L0_xattn_bq': (0.0, 0.8),
     'L0_xattn_bk': (0.0, 0.8),
     'L0_xattn_bv': (0.0, 0.1),
     'L0_xattn_bo': (0.0, 0.1),
     'L0_xattn_ln_gamma': (1.0, 0.6),
     'L0_xattn_ln_beta': (0.0, 0.8),
     'L1_xattn_norm_w': (1.0, 0.6)}
    factors = {}
    for name, (base, spread) in spreads.items():
        noise = np.random.default_rng([zlib.crc32(name.encode()), seed]).standard_normal(out[name].shape)
        drawn = base * np.exp(spread * noise) if base else spread * noise
        out[name] = jnp.asarray(drawn.astype(out[name].dtype))
    for name, factor in factors.items():
        out[name] = (out[name] * factor).astype(out[name].dtype)
    return out
```

```python
from contextlib import ExitStack

import concourse.bass as bass
from concourse import mybir

ALU = mybir.AluOpType
ACT = mybir.ActivationFunctionType
AX = mybir.AxisListType
F32 = mybir.dt.float32
F16 = mybir.dt.float16

P = 128
WSCALE = 64.0
MROW = 1024.0
LN_EPS = 1e-5
Q_EPS = 1e-5
RMS_EPS = 1e-6

FIRST_TURNS = ["K0.0", "K0.1", "V0.0", "V0.1", "V0.2", "xT0", "q0"]
BATCH_TURNS = (
    [f"K1.{j}" for j in range(8)]
    + ["V1.0", "V1.1", "mT0", "V1.2", "V1.3", "V1.4", "V1.5", "O0"]
    + ["K0.0", "K0.1", "V0.0", "V0.1", "V0.2", "xT1", "q1.0", "q1.1", "xT0", "q0", "mT1", "O1"]
)
NEXT_BATCH = ("K0", "V0", "xT0", "q0")
LAST_TURNS = [t for t in BATCH_TURNS if t.split(".")[0] not in NEXT_BATCH]
TURNS = len(BATCH_TURNS) // 2
assert len(BATCH_TURNS) % 2 == 0


def turn(name, b, last=False):
    if b is None:
        n = FIRST_TURNS.index(name)
        return n % 2, n // 2
    n = len(FIRST_TURNS) + (LAST_TURNS if last else BATCH_TURNS).index(name)
    return n % 2, b * TURNS + n // 2


def build(nc, x, ctxT, WqT0, bq, WkT0, bk, WvT0, bv, WoT0, bo, ln_g, ln_b, wq1, wk1, wv1, wo1, norm_w, out):
    B, T, C = x.shape
    S = ctxT.shape[2]
    H = 16
    D1 = wq1.shape[1] // H
    assert C == 2 * P and D1 == 64 and T <= P and 2 * P < S <= 3 * P
    KT = C // P
    CH = [(c * P, min(P, S - c * P)) for c in range(3)]
    G = 4 * T
    LAST = B - 1
    SCALE0 = float(C // H) ** -0.5
    SCALE1 = 1.0 / (WSCALE * WSCALE)

    def is_last(b):
        return isinstance(b, int) and b == LAST

    with ExitStack() as ctx:
        def sb(name, shape, dt):
            return ctx.enter_context(nc.sbuf_tensor(name, shape, dt))

        def sem(name):
            return ctx.enter_context(nc.semaphore(name))

        proj = ctx.enter_context(nc.psum_tensor("proj", [P, 2, 512], F32))
        mps = ctx.enter_context(nc.psum_tensor("mps", [P, 2, 512], F32))
        sps = ctx.enter_context(nc.psum_tensor("sps", [P, 2, 512], F32))
        ops = ctx.enter_context(nc.psum_tensor("ops", [P, 2, 512], F32))

        ident = sb("ident", [P, P], F32)
        ones = sb("ones", [P, P], F32)
        mask = sb("mask", [P, 4], F32)
        wraw0 = sb("wraw0", [P, 10, C], F32)
        wtmp0 = sb("wtmp0", [P, 10, C], F32)
        wt0 = sb("wt0", [P, 10, C], F16)
        wqd0 = sb("wqd0", [P, KT, 4, P], F16)
        wsum = sb("wsum", [P, 4], F32)
        gam = sb("gam", [P, 4], F32)
        thr = sb("thr", [P, 4], F32)
        nthr = sb("nthr", [P, 4], F32)
        wraw1 = sb("wraw1", [P, 2, 2048], F32)
        wh1 = sb("wh1", [P, 4, 2048], F16)
        wl1 = sb("wl1", [P, 4, 2048], F16)
        bqd = sb("bqd", [P, 4], F32)
        bkp = sb("bkp", [P, KT], F32)
        bvp = sb("bvp", [P, 4], F32)
        bob = sb("bob", [P, C], F32)
        lngp = sb("lngp", [P, KT], F32)
        lnbp = sb("lnbp", [P, KT], F32)
        nwp = sb("nwp", [P, KT], F32)

        ctx32 = sb("ctx32", [P, KT, S], F32)
        ctxh = sb("ctxh", [P, KT, S], F16)
        ctxl = sb("ctxl", [P, KT, S], F16)
        k32 = sb("k32", [P, 2, S], F32)
        KA = [sb("KA0", [P, 4, S], F16), sb("KA1", [P, H, S], F16)]
        KB = [sb("KB0", [P, 4, S], F16), sb("KB1", [P, H, S], F16)]
        qA = [sb("qA0", [P, H, T], F16), sb("qA1", [P, H, T], F16)]
        qB = [sb("qB0", [P, H, T], F16), sb("qB1", [P, H, T], F16)]
        V0 = sb("V0", [P, 3, H, 32], F32)
        V1 = sb("V1", [P, 3, 8, 192], F32)
        x32 = sb("x32", [P, C], F32)
        xb = sb("xb", [P, C], F32)
        x1 = sb("x1", [P, C], F32)
        xout = sb("xout", [P, C], F32)
        stats = [sb(f"stats{l}", [P, 6], F32) for l in range(2)]
        mv = [sb(f"mv{l}", [P, 2], F32) for l in range(2)]
        small = [sb(f"small{l}", [P, 8], F32) for l in range(2)]
        xn = [sb(f"xn{l}", [P, C], F32) for l in range(2)]
        xT32 = [sb(f"xT32_{l}", [P, KT, T], F32) for l in range(2)]
        xTh = [sb(f"xTh{l}", [P, KT, T], F16) for l in range(2)]
        xTl = [sb(f"xTl{l}", [P, KT, T], F16) for l in range(2)]
        q32 = sb("q32", [P, 2, 4, T], F32)
        q32_0 = sb("q32_0", [P, 4, T], F32)
        qh0 = sb("qh0", [P, 4, T], F16)
        ql0 = sb("ql0", [P, 4, T], F16)
        gate = sb("gate", [P, 4], F32)
        mx = [sb(f"mx{l}", [P, H], F32) for l in range(2)]
        mT = [sb(f"mT{l}", [P, T], F16) for l in range(2)]
        prob = sb("prob", [P, 4, G], F32)
        rec0 = sb("rec0", [P, 2, 2 * T], F32)
        rcp0 = sb("rcp0", [P, 2, 2 * T], F32)
        on0 = sb("on0", [P, 4, T], F32)
        o32_0 = sb("o32_0", [P, 4, T], F32)
        oh0 = sb("oh0", [P, 4, T], F16)
        ol0 = sb("ol0", [P, 4, T], F16)
        rec1 = sb("rec1", [P, 2, G], F32)
        o32_1 = sb("o32_1", [P, 8, T], F32)
        oh1 = sb("oh1", [P, 8, T], F16)
        ol1 = sb("ol1", [P, 8, T], F16)

        const_in = sem("const_in")
        w0_in = sem("w0_in")
        w1_in = [sem(f"w1_in{i}") for i in range(2)]
        pad_zero = sem("pad_zero")
        setup_pool = sem("setup_pool")
        setup_ones = sem("setup_ones")
        setup_fill = sem("setup_fill")
        w_sum = sem("w_sum")
        gam_mm = sem("gam_mm")
        gam_ok = sem("gam_ok")
        w_step = sem("w_step")
        w0_ok = sem("w0_ok")
        w1_scaled = sem("w1_scaled")
        w1_hi = sem("w1_hi")
        w1_lo = sem("w1_lo")
        proj_full = [sem(f"proj_full{i}") for i in range(2)]
        proj_read = [sem(f"proj_read{i}") for i in range(2)]
        ctx_in = sem("ctx_in")
        ctx_hi = sem("ctx_hi")
        ctx_split = sem("ctx_split")
        k_hi = sem("k_hi")
        k_lo = sem("k_lo")
        kb_in = [sem(f"kb_in{l}") for l in range(2)]
        x_in = sem("x_in")
        xb_ready = sem("xb_ready")
        st_done = [sem(f"st_done{l}") for l in range(2)]
        ag_done = [sem(f"ag_done{l}") for l in range(2)]
        ms_done = sem("ms_done")
        ve_done = [sem(f"ve_done{l}") for l in range(2)]
        ln_done = [sem(f"ln_done{l}") for l in range(2)]
        rs_done = [sem(f"rs_done{l}") for l in range(2)]
        nw_done = [sem(f"nw_done{l}") for l in range(2)]
        xn_ready = [sem(f"xn_ready{l}") for l in range(2)]
        xTh_ready = [sem(f"xTh_ready{l}") for l in range(2)]
        xTl_ready = [sem(f"xTl_ready{l}") for l in range(2)]
        qA1_ready = sem("qA1_ready")
        qB1_ready = sem("qB1_ready")
        qh0_ready = sem("qh0_ready")
        ql0_ready = sem("ql0_ready")
        q0_ready = sem("q0_ready")
        max_full = sem("max_full")
        max_done = sem("max_done")
        mrow_in = [sem(f"mrow_in{l}") for l in range(2)]
        s_full = sem("s_full")
        exp_done = sem("exp_done")
        prob_used = sem("prob_used")
        o_done = sem("o_done")
        shuf_done = sem("shuf_done")
        rcp0_done = sem("rcp0_done")
        o32_0_ready = sem("o32_0_ready")
        oh0_ready = sem("oh0_ready")
        ol0_ready = sem("ol0_ready")
        rec1_done = sem("rec1_done")
        oh1_ready = sem("oh1_ready")
        ol1_ready = sem("ol1_ready")
        out_stored = sem("out_stored")

        N_CONST_DMA = 2 + 1 + 4 + 3 + 1
        N_W0_DMA = 3 + 4

        block = ctx.enter_context(nc.Block())

        def filled(eng, name, b):
            i, before = turn(name, b, is_last(b))
            eng.wait_ge(proj_full[i], before + 1)

        def taken(eng, name, b):
            i, before = turn(name, b, is_last(b))
            eng.wait_ge(proj_read[i], before + 1)

        def heads1(g):
            return [g % 2 + 2 * i for i in range(4 * (g // 2), 4 * (g // 2) + 4)]

        @block.sync
        def _(sp):
            sp.dma_start(ctx32[:], ctxT[0].rearrange("(k p) s -> p k s", p=P)).then_inc(ctx_in, 16)
            sp.dma_start(x32[0:T, :], x[0]).then_inc(x_in, 16)
            for i, w in enumerate((WqT0, WkT0, WvT0)):
                sp.dma_start(wraw0[:, 2 * i:2 * i + 2, :], w.rearrange("(k p) n -> p k n", p=P)).then_inc(w0_in, 16)
            sp.wait_ge(pad_zero, 1)
            wo_heads = WoT0.rearrange("(s j d) n -> j d s n", j=4, d=16)
            for j in range(4):
                sp.dma_start(wraw0[32 * j:32 * j + 16, 6:10, :], wo_heads[j]).then_inc(w0_in, 16)
            for half in range(2):
                sp.dma_start(bqd[64 * half:64 * half + 64, :], bq).then_inc(const_in, 16)
            sp.dma_start(bkp[:], bk).then_inc(const_in, 16)
            for j in range(4):
                sp.dma_start(bvp[32 * j:32 * j + 16, :], bv[j]).then_inc(const_in, 16)
            sp.dma_start(lngp[:], ln_g).then_inc(const_in, 16)
            sp.dma_start(lnbp[:], ln_b).then_inc(const_in, 16)
            sp.dma_start(nwp[:], norm_w).then_inc(const_in, 16)
            sp.dma_start(bob[0:T, :], bo.broadcast_to([T, C])).then_inc(const_in, 16)
            for i, w in enumerate((wk1, wv1, wq1, wo1)):
                if i >= 2:
                    sp.wait_ge(w1_lo, i - 1)
                sp.dma_start(wraw1[:, i % 2, :].rearrange("p (k n) -> p k n", n=w.shape[1]),
                             w.rearrange("(k p) n -> p k n", p=P)).then_inc(w1_in[i % 2], 16)

            def copy_kb(layer, tiles):
                for odd in range(2):
                    r = slice(64 * odd, 64 * odd + 64)
                    sp.dma_start(KB[layer][r, odd:tiles:2, :], KA[layer][r, odd:tiles:2, :]).then_inc(kb_in[layer], 16)

            sp.wait_ge(k_hi, 2)
            sp.wait_ge(setup_fill, 1)
            copy_kb(0, 4)

            def batch(b, last):
                if not last:
                    sp.wait_ge(ctx_split, b + 1)
                    sp.dma_start(ctx32[:], ctxT[b + 1].rearrange("(k p) s -> p k s", p=P)).then_inc(ctx_in, 16)
                taken(sp, "mT0", b)
                for s in range(4):
                    r = 0 if s % 2 else 64
                    sp.dma_start(qB[0][r:r + 1, 4 * s:4 * s + 4, :], mT[0][4 * s:4 * s + 4, :]
                                 ).then_inc(mrow_in[0], 16)
                sp.wait_ge(k_hi, b * 10 + 10)
                copy_kb(1, H)
                if not last:
                    taken(sp, "O0", b)
                    sp.dma_start(x32[0:T, :], x[b + 1]).then_inc(x_in, 16)
                    sp.wait_ge(k_hi, b * 10 + 12)
                    copy_kb(0, 4)
                taken(sp, "mT1", b)
                for odd in range(2):
                    r = 0 if odd else 64
                    sp.dma_start(qB[1][r:r + 1, odd:H:2, :], mT[1][odd:H:2, :]).then_inc(mrow_in[1], 16)
                taken(sp, "O1", b)
                sp.dma_start(out[b], xout[0:T, :]).then_inc(out_stored, 16)

            with sp.Fori(0, B - 1) as b:
                batch(b, False)
            batch(LAST, True)
            sp.wait_ge(out_stored, 16 * B + 16)

        @block.tensor
        def _(pe):
            def take(name, b):
                i, before = turn(name, b, is_last(b))
                pe.wait_ge(proj_read[i], before)
                return proj[:, i, :], proj_full[i]

            bank, full = proj[:, 0, :], gam_mm
            pe.wait_ge(setup_ones, 1)
            pe.wait_ge(w_sum, 4)
            pe.matmul(bank[:, 0:4], ones[:], wsum[:], start=True, stop=True).then_inc(full, 1)

            def keys0(nb, b):
                for t in range(2):
                    bank, full = take(f"K0.{t}", b)
                    for n, (k, c) in enumerate((k, c) for k in range(KT) for c in (ctxh, ctxl)):
                        mm = pe.matmul(bank[:, 0:S], wt0[:, 2 + k, P * t:P * t + P], c[:, k, :],
                                       start=n == 0, stop=n == 2 * KT - 1)
                    mm.then_inc(full, 1)

            def values0(nb, b):
                for c, (at, rows) in enumerate(CH):
                    bank, full = take(f"V0.{c}", b)
                    for n, (k, cc) in enumerate((k, cc) for k in range(KT) for cc in (ctxh, ctxl)):
                        mm = pe.matmul(bank[0:rows, 0:C], cc[:, k, at:at + rows], wt0[:, 4 + k, :],
                                       start=n == 0, stop=n == 2 * KT - 1)
                    mm.then_inc(full, 1)

            def transpose_x(layer, nb, b):
                bank, full = take(f"xT{layer}", b)
                pe.wait_ge(xn_ready[layer], nb + 1)
                for k in range(KT):
                    mm = pe.transpose(bank[:, T * k:T * k + T], xn[layer][0:T, P * k:P * k + P], ident[0:T, 0:T])
                mm.then_inc(full, 1)

            def queries0(nb, b):
                bank, full = take("q0", b)
                pe.wait_ge(xTl_ready[0], nb + 1)
                for s in range(4):
                    for n, (k, xx) in enumerate((k, xx) for k in range(KT) for xx in (xTh[0], xTl[0])):
                        mm = pe.matmul(bank[:, T * s:T * s + T], wqd0[:, k, s, :], xx[:, k, :],
                                       start=n == 0, stop=n == 2 * KT - 1)
                mm.then_inc(full, 1)

            def three(k, wi, cols, data_h, data_l):
                h, l = wh1[:, wi, :], wl1[:, wi, :]
                at = 1024 * k
                w = slice(at + cols[0], at + cols[1])
                return [(h[:, w], data_h), (h[:, w], data_l), (l[:, w], data_h)]

            def key_tile1(j, b):
                bank, full = take(f"K1.{j}", b)
                pairs = [p for k in range(KT) for p in three(k, 0, (P * j, P * j + P), ctxh[:, k, :], ctxl[:, k, :])]
                for n, (w, c) in enumerate(pairs):
                    mm = pe.matmul(bank[:, 0:S], w, c, start=n == 0, stop=n == len(pairs) - 1)
                mm.then_inc(full, 1)

            def value_tile1(u, b):
                bank, full = take(f"V1.{u}", b)
                at, rows = CH[u // 2]
                cols = (512 * (u % 2), 512 * (u % 2) + 512)
                pairs = [p for k in range(KT)
                         for p in three(k, 1, cols, ctxh[:, k, at:at + rows], ctxl[:, k, at:at + rows])]
                for n, (w, c) in enumerate(pairs):
                    mm = pe.matmul(bank[0:rows, :], c, w, start=n == 0, stop=n == len(pairs) - 1)
                mm.then_inc(full, 1)

            def queries1(b):
                pe.wait_ge(xTl_ready[1], b + 1)
                for half in range(2):
                    bank, full = take(f"q1.{half}", b)
                    for i in range(4):
                        j = 4 * half + i
                        pairs = [p for k in range(KT)
                                 for p in three(k, 2, (P * j, P * j + P), xTh[1][:, k, :], xTl[1][:, k, :])]
                        for n, (w, xx) in enumerate(pairs):
                            mm = pe.matmul(bank[:, T * i:T * i + T], w, xx, start=n == 0, stop=n == len(pairs) - 1)
                    mm.then_inc(full, 1)

            def row_scores(layer, h, b):
                n = H * layer + h
                if h >= 2:
                    pe.wait_ge(max_done, b * 2 * H + n - 1)
                tile = KA[layer][:, h if layer else h // 4, :]
                pe.matmul(mps[0:T, n % 2, 0:S], qA[layer][:, h, :], tile, start=True, stop=True).then_inc(max_full, 1)

            def transpose_max(layer, b):
                bank, full = take(f"mT{layer}", b)
                pe.wait_ge(max_done, b * 2 * H + H * (layer + 1))
                pe.transpose(bank[0:H, 0:T], mx[layer][0:T, :], ident[0:T, 0:T]).then_inc(full, 1)

            def scores(layer, u, b):
                n = 12 * layer + u
                g, c = u // 3, u % 3
                at, rows = CH[c]
                if u >= 2:
                    pe.wait_ge(exp_done, b * 24 + n - 1)
                if layer == 0:
                    pe.matmul(sps[0:rows, n % 2, 0:G], KA[0][:, g, at:at + rows],
                              qA[0][:, 4 * g:4 * g + 4, :], start=True, stop=False)
                    mm = pe.matmul(sps[0:rows, n % 2, 0:G], KB[0][:, g, at:at + rows],
                                   qB[0][:, 4 * g:4 * g + 4, :], start=False, stop=True)
                else:
                    for i, h in enumerate(heads1(g)):
                        o = sps[0:rows, n % 2, T * i:T * i + T]
                        pe.matmul(o, KA[1][:, h, at:at + rows], qA[1][:, h, :], start=True, stop=False)
                        mm = pe.matmul(o, KB[1][:, h, at:at + rows], qB[1][:, h, :], start=False, stop=True)
                mm.then_inc(s_full, 1)

            def weigh(layer, u, b):
                n = 12 * layer + u
                g, c = u // 3, u % 3
                rows = CH[c][1]
                pe.wait_ge(exp_done, b * 24 + n + 1)
                p = prob[0:rows, n % 4, :]
                if layer == 0:
                    for j in range(4):
                        mm = pe.matmul(ops[32 * j:32 * j + 32, g // 2, T * (g % 2):T * (g % 2) + T],
                                       V0[0:rows, c, 4 * g + j, :], p[:, T * j:T * j + T],
                                       start=c == 0, stop=c == 2, tile_position=(0, 32 * j))
                else:
                    if c == 0 and g >= 2:
                        pe.wait_ge(o_done, b * 6 + g + 1)
                    for i, h in enumerate(heads1(g)):
                        w = V1[0:rows, c, h // 2, 64 * (h % 2):64 * (h % 2) + P]
                        mm = pe.matmul(ops[:, g % 2, T * i:T * i + T], w, p[:, T * i:T * i + T],
                                       start=c == 0 and i == 0, stop=c == 2, skip_group_check=True)
                mm.then_inc(prob_used, 1)

            def attend(layer, b):
                scores(layer, 0, b)
                scores(layer, 1, b)
                for u in range(12):
                    weigh(layer, u, b)
                    if u < 10:
                        scores(layer, u + 2, b)

            def project_out(layer, b):
                bank, full = take(f"O{layer}", b)
                if layer == 0:
                    pe.wait_ge(ol0_ready, b + 1)
                    for n, (s, oo) in enumerate((s, oo) for s in range(4) for oo in (oh0, ol0)):
                        mm = pe.matmul(bank[0:T, 0:C], oo[:, s, :], wt0[:, 6 + s, :], start=n == 0, stop=n == 7)
                else:
                    pe.wait_ge(ol1_ready, b * 4 + 4)
                    for k in range(8):
                        w = slice(C * k, C * k + C)
                        for n, (oo, ww) in enumerate(((oh1, wh1), (oh1, wl1), (ol1, wh1))):
                            mm = pe.matmul(bank[0:T, 0:C], oo[:, k, :], ww[:, 3, w],
                                           start=k == 0 and n == 0, stop=k == 7 and n == 2)
                mm.then_inc(full, 1)

            pe.wait_ge(w0_ok, 1)
            pe.wait_ge(ctx_split, 1)
            keys0(0, None)
            values0(0, None)
            pe.wait_ge(setup_pool, 7)
            transpose_x(0, 0, None)
            queries0(0, None)
            pe.wait_ge(w1_lo, 4)
            pe.wait_ge(setup_fill, 1)

            def batch(b, last):
                pe.wait_ge(k_lo, b * 20 + 4)
                pe.wait_ge(q0_ready, b + 1)
                for j in range(8):
                    key_tile1(j, b)
                    row_scores(0, 2 * j, b)
                    row_scores(0, 2 * j + 1, b)
                value_tile1(0, b)
                value_tile1(1, b)
                transpose_max(0, b)
                value_tile1(2, b)
                pe.wait_ge(mrow_in[0], b * 64 + 64)
                pe.wait_ge(kb_in[0], b * 32 + 32)
                attend(0, b)
                for u in range(3, 6):
                    value_tile1(u, b)
                project_out(0, b)
                if not last:
                    pe.wait_ge(ctx_split, b + 2)
                    keys0(b + 1, b)
                    values0(b + 1, b)
                transpose_x(1, b, b)
                queries1(b)
                if not last:
                    transpose_x(0, b + 1, b)
                pe.wait_ge(k_lo, b * 20 + 20)
                pe.wait_ge(qA1_ready, b * 2 + 2)
                for h in range(10):
                    row_scores(1, h, b)
                if not last:
                    queries0(b + 1, b)
                for h in range(10, H):
                    row_scores(1, h, b)
                transpose_max(1, b)
                pe.wait_ge(mrow_in[1], b * 32 + 32)
                pe.wait_ge(qB1_ready, b * 4 + 4)
                pe.wait_ge(kb_in[1], b * 32 + 32)
                attend(1, b)
                project_out(1, b)

            with pe.Fori(0, B - 1) as b:
                batch(b, False)
            batch(LAST, True)

        @block.scalar
        def _(act):
            def full(name, b):
                i, before = turn(name, b, is_last(b))
                act.wait_ge(proj_full[i], before + 1)
                return proj[:, i, :], proj_read[i]

            def key_tile(name, n, scale, bias, b):
                bank, free = full(name, b)
                if not isinstance(n, int) or n >= 2:
                    act.wait_ge(k_lo, n * 2 - 2)
                slot = k32[:, int(name[-1]) % 2, :]
                nc.scalar.activation(slot, bank[:, 0:S], ACT.Identity, scale=scale, bias=bias
                                     ).then_inc(free, 1)

            def values0(c, nb, b):
                bank, free = full(f"V0.{c}", b)
                rows = CH[c][1]
                nc.scalar.activation(V0[0:rows, c, :, 0:16], bank[0:rows, 0:C].rearrange("p (h d) -> p h d", d=16),
                                     ACT.Copy).then_inc(free, 1)

            def values1(u, b):
                bank, free = full(f"V1.{u}", b)
                rows = CH[u // 2][1]
                at = 4 * (u % 2)
                dst = V1[0:rows, u // 2, at:at + 4, :].rearrange("p j (w d) -> p j w d", d=64)[:, :, 0:3:2, :]
                src = bank[0:rows, :].rearrange("p (j w d) -> p j w d", w=2, d=64)
                nc.scalar.activation(dst, src, ACT.Copy).then_inc(free, 1)

            def row_max(layer, b):
                bank, free = full(f"mT{layer}", b)
                nc.scalar.activation(mT[layer][0:H, :], bank[0:H, 0:T], ACT.Copy, scale=-1.0 / MROW
                                     ).then_inc(free, 1)

            def rsqrt(layer, nb):
                act.wait_ge(ve_done[layer], nb + 1)
                s = small[layer]
                nc.scalar.activation(s[0:T, 1:2], s[0:T, 0:1], ACT.Ln).then_inc(ln_done[layer], 1)
                act.wait_ge(ln_done[layer], nb + 1)
                nc.scalar.activation(s[0:T, 2:3], s[0:T, 1:2], ACT.Exp, scale=-0.5).then_inc(rs_done[layer], 1)

            def transposed_x(layer, nb, b):
                bank, free = full(f"xT{layer}", b)
                if layer == 0:
                    for k in range(KT):
                        i = nc.scalar.activation(xT32[0][:, k, :], bank[:, T * k:T * k + T], ACT.Identity,
                                                 scale=lngp[:, k:k + 1], bias=lnbp[:, k:k + 1])
                else:
                    for k in range(KT):
                        i = nc.scalar.activation(xT32[1][:, k, :], bank[:, T * k:T * k + T], ACT.Identity,
                                                 scale=nwp[:, k:k + 1])
                i.then_inc(free, 1)

            def queries0(nb, b):
                bank, free = full("q0", b)
                for s in range(4):
                    i = nc.scalar.activation(q32_0[:, s, :], bank[:, T * s:T * s + T], ACT.Identity,
                                             scale=gam[:, 0:1], bias=bqd[:, s:s + 1])
                i.then_inc(free, 1)

            def exps(layer, b):
                for u in range(12):
                    n = 12 * layer + u
                    rows = CH[u % 3][1]
                    act.wait_ge(s_full, b * 24 + n + 1)
                    if u >= 4:
                        act.wait_ge(prob_used, b * 24 + n - 3)
                    nc.scalar.activation(prob[0:rows, n % 4, :], sps[0:rows, n % 2, 0:G], ACT.Exp,
                                         scale=SCALE1 if layer else SCALE0).then_inc(exp_done, 1)

            act.wait_ge(const_in, 16 * N_CONST_DMA)
            act.wait_ge(gam_ok, 1)
            for t in range(2):
                key_tile(f"K0.{t}", t, gam[:, 1:2], bkp[:, t:t + 1], None)
            for c in range(3):
                values0(c, 0, None)
            rsqrt(0, 0)
            transposed_x(0, 0, None)
            queries0(0, None)

            def batch(b, last):
                for j in range(8):
                    key_tile(f"K1.{j}", b * 10 + 2 + j, 1.0, 0.0, b)
                values1(0, b)
                values1(1, b)
                row_max(0, b)
                values1(2, b)
                exps(0, b)
                for u in range(3, 6):
                    values1(u, b)
                act.wait_ge(o_done, b * 6 + 2)
                for s in range(4):
                    i = nc.scalar.activation(o32_0[:, s, :], on0[:, s, :], ACT.Identity,
                                             scale=gam[:, 2:3], bias=bvp[:, s:s + 1])
                i.then_inc(o32_0_ready, 1)
                if not last:
                    for t in range(2):
                        key_tile(f"K0.{t}", b * 10 + 10 + t, gam[:, 1:2], bkp[:, t:t + 1], b)
                        if t == 0:
                            rsqrt(1, b)
                    for c in range(3):
                        values0(c, b + 1, b)
                else:
                    rsqrt(1, b)
                transposed_x(1, b, b)
                for half in range(2):
                    bank, free = full(f"q1.{half}", b)
                    nc.scalar.activation(q32[:, half, :, :], bank[:, 0:G].rearrange("p (j t) -> p j t", t=T),
                                         ACT.Copy).then_inc(free, 1)
                if not last:
                    rsqrt(0, b + 1)
                    transposed_x(0, b + 1, b)
                    queries0(b + 1, b)
                row_max(1, b)
                exps(1, b)

            with act.Fori(0, B - 1) as b:
                batch(b, False)
            batch(LAST, True)

        @block.vector
        def _(dve):
            steps = [0]

            def step(ins):
                steps[0] += 1
                ins.then_inc(w_step, 1)
                dve.wait_ge(w_step, steps[0])

            def split_ctx_hi(nb):
                dve.wait_ge(ctx_in, nb * 16 + 16)
                nc.vector.tensor_copy(ctxh[:], ctx32[:]).then_inc(ctx_hi, 1)

            def key_tile(layer, t, name, b):
                taken(dve, name, b)
                slot = t % 2
                nc.vector.tensor_copy(KA[layer][0:64, 2 * t, :], k32[0:64, slot, :])
                nc.vector.tensor_copy(KA[layer][64:P, 2 * t + 1, :], k32[64:P, slot, :]).then_inc(k_hi, 1)

            def statistics(layer, nb):
                src = x1 if layer else x32
                nc.vector.bn_stats(out=stats[layer][0:T, :], in_=src[0:T, :]).then_inc(st_done[layer], 1)
                dve.wait_ge(st_done[layer], nb + 1)
                nc.vector.memset(gate[0:1, layer:layer + 1], 0.0)
                m = mv[layer]
                nc.vector.bn_aggr(out=m[0:T, :], in_=stats[layer][0:T, :]).then_inc(ag_done[layer], 1)
                dve.wait_ge(ag_done[layer], nb + 1)
                s = small[layer]
                var = m[0:T, 1:2]
                if layer:
                    nc.vector.scalar_tensor_tensor(out=s[0:T, 3:4], in0=m[0:T, 0:1], scalar=m[0:T, 0:1],
                                                   in1=m[0:T, 1:2], op0=ALU.mult, op1=ALU.add).then_inc(ms_done, 1)
                    dve.wait_ge(ms_done, nb + 1)
                    var = s[0:T, 3:4]
                nc.vector.tensor_scalar(s[0:T, 0:1], var, RMS_EPS if layer else LN_EPS, None, ALU.add
                                        ).then_inc(ve_done[layer], 1)

            def normalise_x(layer, nb):
                s, n = small[layer], nw_done[layer]
                y = s[0:T, 2:3]
                dve.wait_ge(rs_done[layer], nb + 1)
                nc.vector.tensor_tensor(s[0:T, 4:5], y, y, ALU.mult).then_inc(n, 1)
                dve.wait_ge(n, nb * 3 + 1)
                nc.vector.tensor_scalar(s[0:T, 5:6], s[0:T, 4:5], s[0:T, 0:1], -0.5, ALU.mult, ALU.mult).then_inc(n, 1)
                dve.wait_ge(n, nb * 3 + 2)
                nc.vector.tensor_scalar(s[0:T, 6:7], s[0:T, 5:6], 1.5, y, ALU.add, ALU.mult).then_inc(n, 1)
                dve.wait_ge(n, nb * 3 + 3)
                if layer:
                    i = nc.vector.tensor_scalar(xn[1][0:T, :], x1[0:T, :], s[0:T, 6:7], None, ALU.mult)
                else:
                    i = nc.vector.tensor_scalar(xn[0][0:T, :], x32[0:T, :], mv[0][0:T, 0:1], s[0:T, 6:7],
                                                ALU.subtract, ALU.mult)
                i.then_inc(xn_ready[layer], 1)

            def x_hi(layer, b):
                taken(dve, f"xT{layer}", b)
                nc.vector.tensor_copy(xTh[layer][:], xT32[layer][:]).then_inc(xTh_ready[layer], 1)

            def queries0_hi(nb, b):
                taken(dve, "q0", b)
                nc.vector.tensor_copy(qh0[:], q32_0[:]).then_inc(qh0_ready, 1)
                dve.wait_ge(qh0_ready, nb + 1)
                for j in range(4):
                    nc.vector.tensor_scalar(qA[0][:, j:H:4, :], qh0[:], mask[:, j:j + 1], None, ALU.mult)

            def queries0_lo(nb):
                dve.wait_ge(ql0_ready, nb + 1)
                for j in range(4):
                    for odd in range(2):
                        r = slice(64 * odd, 64 * odd + 64)
                        i = nc.vector.tensor_scalar(qB[0][r, 4 * odd + j:H:8, :], ql0[r, odd:4:2, :],
                                                    mask[r, j:j + 1], None, ALU.mult)
                i.then_inc(q0_ready, 1)

            def queries1_hi(half, b):
                taken(dve, f"q1.{half}", b)
                for odd in range(2):
                    r = slice(64 * odd, 64 * odd + 64)
                    for to in range(2):
                        i = nc.vector.tensor_copy(qA[1][64 * to:64 * to + 64, 8 * half + odd:8 * half + 8:2, :],
                                                  q32[r, half, :, :])
                i.then_inc(qA1_ready, 1)

            def row_max(layer, h, b):
                n = H * layer + h
                dve.wait_ge(max_full, b * 2 * H + n + 1)
                nc.vector.tensor_reduce(mx[layer][0:T, h:h + 1], mps[0:T, n % 2, 0:S], AX.X, ALU.max
                                        ).then_inc(max_done, 1)

            def normalise0(i, b):
                dve.wait_ge(prob_used, b * 24 + 6 * i + 6)
                nc.vector.memset(gate[0:1, 2 + i:3 + i], 0.0)
                src = ops[:, i, 0:2 * T]
                nc.vector.stream_shuffle(rec0[:, i, :], src, list(range(16, 32)) * 2).then_inc(shuf_done, 1)
                dve.wait_ge(shuf_done, b * 2 + i + 1)
                nc.vector.reciprocal(rcp0[:, i, :], rec0[:, i, :]).then_inc(rcp0_done, 1)
                dve.wait_ge(rcp0_done, b * 2 + i + 1)
                nc.vector.tensor_tensor(on0[:, 2 * i:2 * i + 2, :], src.rearrange("p (s t) -> p s t", t=T),
                                        rcp0[:, i, :].rearrange("p (s t) -> p s t", t=T), ALU.mult).then_inc(o_done, 1)

            def normalise1(g, b):
                dve.wait_ge(prob_used, b * 24 + 12 + 3 * g + 3)
                odd = g % 2
                r = slice(64 * odd, 64 * odd + 64)
                den = slice(64 - 64 * odd, P - 64 * odd)
                at = 4 * (g // 2)
                nc.vector.reciprocal(rec1[r, odd, :], ops[den, odd, 0:G]).then_inc(rec1_done, 1)
                dve.wait_ge(rec1_done, b * 4 + g + 1)
                nc.vector.tensor_tensor(o32_1[r, at:at + 4, :], ops[r, odd, 0:G].rearrange("p (j t) -> p j t", t=T),
                                        rec1[r, odd, :].rearrange("p (j t) -> p j t", t=T), ALU.mult
                                        ).then_inc(o_done, 1)
                dve.wait_ge(o_done, b * 6 + 2 + g + 1)
                nc.vector.tensor_copy(oh1[r, at:at + 4, :], o32_1[r, at:at + 4, :]).then_inc(oh1_ready, 1)

            step(nc.vector.memset(wraw0[:, 6:10, :], 0.0))
            nc.vector.memset(bvp[:], 0.0).then_inc(pad_zero, 1)
            nc.vector.memset(gate[:], 0.0).then_inc(out_stored, 16)
            nc.vector.memset(ones[:], 1.0).then_inc(setup_ones, 1)
            split_ctx_hi(0)
            dve.wait_ge(w0_in, 16 * N_W0_DMA)
            for i, (a, z) in enumerate(((0, 2), (2, 4), (4, 6), (6, 10))):
                nc.vector.tensor_reduce(wsum[:, i:i + 1], wraw0[:, a:z, :], AX.XY, ALU.add,
                                        apply_absolute_value=True).then_inc(w_sum, 1)
            dve.wait_ge(gam_mm, 1)
            step(nc.vector.tensor_scalar(gam[:], proj[:, 0, 0:4], 1.0 / (C * C), None, ALU.mult))
            step(nc.vector.tensor_scalar(thr[:], gam[:], Q_EPS, 0.5, ALU.add, ALU.mult))
            nc.vector.tensor_scalar(nthr[:], thr[:], -1.0, None, ALU.mult).then_inc(gam_ok, 1)
            dve.wait_ge(gam_ok, 1)
            for i, (a, z) in enumerate(((0, 2), (2, 4), (4, 6), (6, 10))):
                step(nc.vector.tensor_scalar(wtmp0[:, a:z, :], wraw0[:, a:z, :], nthr[:, i:i + 1], None, ALU.is_lt))
                step(nc.vector.scalar_tensor_tensor(out=wt0[:, a:z, :], in0=wraw0[:, a:z, :], scalar=thr[:, i:i + 1],
                                                    in1=wtmp0[:, a:z, :], op0=ALU.is_gt, op1=ALU.subtract))
            for k in range(KT):
                for half in range(2):
                    i = nc.vector.tensor_copy(wqd0[:, k, :, 64 * half:64 * half + 64],
                                              wt0[:, k, :].rearrange("p (s d) -> p s d", d=64))
            i.then_inc(w0_ok, 1)
            dve.wait_ge(x_in, 16)
            statistics(0, 0)
            for t in range(2):
                key_tile(0, t, f"K0.{t}", None)
            normalise_x(0, 0)
            x_hi(0, None)
            dve.wait_ge(setup_pool, 7)
            for layer in range(2):
                nc.vector.memset(KB[layer][:], 0.0)
                step(nc.vector.memset(qB[layer][:], 0.0))
                nc.vector.memset(KB[layer][64:65, 0::2, :], MROW)
                nc.vector.memset(KB[layer][0:1, 1::2, :], MROW)
            nc.vector.memset(V0[:, :, :, 16:32], 1.0)
            nc.vector.memset(V1[:, :, :, 64:P], 1.0).then_inc(setup_fill, 1)
            for i in range(4):
                dve.wait_ge(w1_in[i % 2], 16 * (i // 2 + 1))
                nc.vector.tensor_scalar(wraw1[:, i % 2, :], wraw1[:, i % 2, :], WSCALE, None, ALU.mult
                                        ).then_inc(w1_scaled, 1)
                dve.wait_ge(w1_scaled, i + 1)
                nc.vector.tensor_copy(wh1[:, i, :], wraw1[:, i % 2, :]).then_inc(w1_hi, 1)
            queries0_hi(0, None)
            queries0_lo(0)

            def batch(b, last):
                for j in range(8):
                    key_tile(1, j, f"K1.{j}", b)
                    row_max(0, 2 * j, b)
                    row_max(0, 2 * j + 1, b)
                normalise0(0, b)
                normalise0(1, b)
                dve.wait_ge(o32_0_ready, b + 1)
                nc.vector.tensor_copy(oh0[:], o32_0[:]).then_inc(oh0_ready, 1)
                if not last:
                    filled(dve, "V1.5", b)
                    split_ctx_hi(b + 1)
                filled(dve, "O0", b)
                dve.wait_ge(xb_ready, b + 1)
                i, before = turn("O0", b, last)
                nc.vector.scalar_tensor_tensor(out=x1[0:T, :], in0=proj[0:T, i, 0:C], scalar=gam[0:T, 3:4],
                                               in1=xb[0:T, :], op0=ALU.mult, op1=ALU.add).then_inc(proj_read[i], 1)
                taken(dve, "O0", b)
                statistics(1, b)
                if not last:
                    key_tile(0, 0, "K0.0", b)
                normalise_x(1, b)
                if not last:
                    key_tile(0, 1, "K0.1", b)
                x_hi(1, b)
                if not last:
                    dve.wait_ge(x_in, b * 16 + 32)
                    statistics(0, b + 1)
                for half in range(2):
                    queries1_hi(half, b)
                if not last:
                    normalise_x(0, b + 1)
                for h in range(6):
                    row_max(1, h, b)
                if not last:
                    x_hi(0, b)
                for h in range(6, H):
                    row_max(1, h, b)
                if not last:
                    queries0_hi(b + 1, b)
                    queries0_lo(b + 1)
                for g in range(4):
                    normalise1(g, b)
                filled(dve, "O1", b)
                dve.wait_ge(out_stored, b * 16 + 16)
                i, before = turn("O1", b, last)
                nc.vector.scalar_tensor_tensor(out=xout[0:T, :], in0=proj[0:T, i, 0:C], scalar=SCALE1,
                                               in1=x1[0:T, :], op0=ALU.mult, op1=ALU.add).then_inc(proj_read[i], 1)

            with dve.Fori(0, B - 1) as b:
                batch(b, False)
            batch(LAST, True)

        @block.gpsimd
        def _(pool):
            def setup(ins, n):
                ins.then_inc(setup_pool, 1)
                pool.wait_ge(setup_pool, n)

            setup(nc.gpsimd.memset(ident[:], 0.0), 1)
            setup(nc.gpsimd.memset(mask[:], 1.0), 2)
            setup(nc.gpsimd.affine_select(out=ident[:], in_=ident[:], compare_op=ALU.not_equal, fill=1.0, base=0,
                                          pattern=[[-1, P]], channel_multiplier=1), 3)
            for half in range(2):
                m = mask[64 * half:64 * half + 64, :]
                setup(nc.gpsimd.affine_select(out=m, in_=m, compare_op=ALU.is_ge, fill=0.0, base=0,
                                              pattern=[[-16, 4]], channel_multiplier=1), 4 + 2 * half)
                setup(nc.gpsimd.affine_select(out=m, in_=m, compare_op=ALU.is_ge, fill=0.0, base=15,
                                              pattern=[[16, 4]], channel_multiplier=-1), 5 + 2 * half)

            def lo_part(out, a, hi, done, count):
                nc.gpsimd.tensor_tensor(out, a, hi, ALU.subtract).then_inc(done, 1)
                pool.wait_ge(done, count)

            def split_ctx_lo(nb):
                pool.wait_ge(ctx_hi, nb + 1)
                lo_part(ctxl[:], ctx32[:], ctxh[:], ctx_split, nb + 1)

            def key_tile(layer, t, n):
                pool.wait_ge(k_hi, n + 1)
                slot = k32[:, t % 2, :]
                k = KA[layer]
                lo_part(k[64:P, 2 * t, :], slot[0:64, :], k[0:64, 2 * t, :], k_lo, n * 2 + 1)
                lo_part(k[0:64, 2 * t + 1, :], slot[64:P, :], k[64:P, 2 * t + 1, :], k_lo, n * 2 + 2)

            def x_lo(layer, nb):
                pool.wait_ge(xTh_ready[layer], nb + 1)
                lo_part(xTl[layer][:], xT32[layer][:], xTh[layer][:], xTl_ready[layer], nb + 1)

            def queries0_lo(nb):
                pool.wait_ge(qh0_ready, nb + 1)
                lo_part(ql0[:], q32_0[:], qh0[:], ql0_ready, nb + 1)

            split_ctx_lo(0)
            for t in range(2):
                key_tile(0, t, t)
            x_lo(0, 0)
            for i in range(4):
                pool.wait_ge(w1_hi, i + 1)
                lo_part(wl1[:, i, :], wraw1[:, i % 2, :], wh1[:, i, :], w1_lo, i + 1)
            queries0_lo(0)
            pool.wait_ge(const_in, 16 * N_CONST_DMA)

            def batch(b, last):
                pool.wait_ge(x_in, b * 16 + 16)
                nc.gpsimd.tensor_tensor(xb[0:T, :], x32[0:T, :], bob[0:T, :], ALU.add).then_inc(xb_ready, 1)
                pool.wait_ge(xb_ready, b + 1)
                for j in range(8):
                    key_tile(1, j, b * 10 + 2 + j)
                pool.wait_ge(oh0_ready, b + 1)
                lo_part(ol0[:], o32_0[:], oh0[:], ol0_ready, b + 1)
                if not last:
                    split_ctx_lo(b + 1)
                    key_tile(0, 0, b * 10 + 10)
                    key_tile(0, 1, b * 10 + 11)
                x_lo(1, b)
                for half in range(2):
                    pool.wait_ge(qA1_ready, b * 2 + half + 1)
                    for odd in range(2):
                        r = slice(64 * odd, 64 * odd + 64)
                        heads = slice(8 * half + odd, 8 * half + 8, 2)
                        lo_part(qB[1][r, heads, :], q32[r, half, :, :], qA[1][r, heads, :],
                                qB1_ready, b * 4 + 2 * half + odd + 1)
                if not last:
                    x_lo(0, b + 1)
                    queries0_lo(b + 1)
                for g in range(4):
                    pool.wait_ge(oh1_ready, b * 4 + g + 1)
                    r = slice(64 * (g % 2), 64 * (g % 2) + 64)
                    at = 4 * (g // 2)
                    lo_part(ol1[r, at:at + 4, :], o32_1[r, at:at + 4, :], oh1[r, at:at + 4, :],
                            ol1_ready, b * 4 + g + 1)

            with pool.Fori(0, B - 1) as b:
                batch(b, False)
            batch(LAST, True)


def kernel(x, ctx_1024, L0_xattn_Wq, L0_xattn_bq, L0_xattn_Wk, L0_xattn_bk, L0_xattn_Wv, L0_xattn_bv, L0_xattn_Wo,
           L0_xattn_bo, L0_xattn_ln_gamma, L0_xattn_ln_beta, L1_xattn_wq, L1_xattn_wk, L1_xattn_wv, L1_xattn_wo,
           L1_xattn_norm_w):
    import numpy as np
    import concourse.bacc as bacc
    from concourse.bass_utils import run_bass_kernel_spmd

    def by_partition(v):
        return np.asarray(v).reshape(2, P).T

    laid = {
        "x": x, "ctxT": np.asarray(ctx_1024).transpose(0, 2, 1),
        "WqT0": np.asarray(L0_xattn_Wq).T, "bq": np.asarray(L0_xattn_bq).reshape(4, 64).T,
        "WkT0": np.asarray(L0_xattn_Wk).T, "bk": by_partition(L0_xattn_bk),
        "WvT0": np.asarray(L0_xattn_Wv).T, "bv": np.asarray(L0_xattn_bv).reshape(4, 4, 16).transpose(1, 2, 0),
        "WoT0": np.asarray(L0_xattn_Wo).T, "bo": np.asarray(L0_xattn_bo).reshape(1, -1),
        "ln_g": by_partition(L0_xattn_ln_gamma), "ln_b": by_partition(L0_xattn_ln_beta),
        "wq1": L1_xattn_wq, "wk1": L1_xattn_wk, "wv1": L1_xattn_wv, "wo1": L1_xattn_wo,
        "norm_w": by_partition(L1_xattn_norm_w),
    }
    nc = bacc.Bacc("TRN2", target_bir_lowering=False, num_devices=1)
    arrays, args = {}, []
    for name, a in laid.items():
        a = np.ascontiguousarray(a)
        arrays[f"in_{name}"] = a
        args.append(nc.dram_tensor(f"in_{name}", a.shape, mybir.dt.from_np(a.dtype), kind="ExternalInput").ap())
    y = nc.dram_tensor("out_0", tuple(laid["x"].shape), F32, kind="ExternalOutput").ap()
    build(nc, *args, y)
    r = run_bass_kernel_spmd(nc, [arrays], core_ids=[0])
    return r.results[0]["out_0"]
```

```python
from contextlib import ExitStack

import concourse.bass as bass
from concourse import mybir

ALU = mybir.AluOpType
ACT = mybir.ActivationFunctionType
AX = mybir.AxisListType
F32 = mybir.dt.float32
F16 = mybir.dt.float16

P = 128
WSCALE = 64.0
MROW = 1024.0
LN_EPS = 1e-5
Q_EPS = 1e-5
RMS_EPS = 1e-6

BODY_TURNS = (
    ["K0.0", "K0.1", "V0.0", "V0.1", "V0.2", "mT1", "mT0", "xT0", "q0", "O1"]
    + [f"K1.{j}" for j in range(6)] + ["O0", "K1.6", "K1.7"]
    + ["V1.0", "xT1", "V1.1", "V1.2", "V1.3", "q1.0", "q1.1", "V1.4", "V1.5"]
)
LAYER1 = ("mT1", "O1")
AHEAD = ("xT0", "q0")
FIRST_TURNS = list(AHEAD) + [t for t in BODY_TURNS if t not in LAYER1]
NEAR_LAST_TURNS = [t for t in BODY_TURNS if t not in AHEAD]
TURNS = len(BODY_TURNS)
assert TURNS % 2 == 0 and len(FIRST_TURNS) == TURNS


def turn(name, batch, last):
    fixed = isinstance(batch, int)
    if name in LAYER1:
        if fixed and batch == last:
            n = last * TURNS + len(NEAR_LAST_TURNS) + LAYER1.index(name)
            return n % 2, n // 2
        body = batch
    elif name in AHEAD:
        if fixed and batch < 2:
            n = FIRST_TURNS.index(name) if batch == 0 else len(AHEAD) + FIRST_TURNS[len(AHEAD):].index(name)
            return n % 2, n // 2
        body = batch - 2
    else:
        if fixed and batch == 0:
            n = len(AHEAD) + FIRST_TURNS[len(AHEAD):].index(name)
            return n % 2, n // 2
        body = batch - 1
    near_last = fixed and isinstance(body, int) and body == last - 1
    n = (NEAR_LAST_TURNS if near_last else BODY_TURNS).index(name)
    return n % 2, (body + 1) * (TURNS // 2) + n // 2


def build(nc, x, ctxT, WqT0, bq, WkT0, bk, WvT0, bv, WoT0, bo, ln_g, ln_b, wq1, wk1, wv1, wo1, norm_w, out):
    B, T, C = x.shape
    S = ctxT.shape[2]
    H = 16
    D1 = wq1.shape[1] // H
    assert C == 2 * P and D1 == 64 and T <= P and 2 * P < S <= 3 * P
    KT = C // P
    CH = [(c * P, min(P, S - c * P)) for c in range(3)]
    G = 4 * T
    LAST = B - 1
    SCALE0 = float(C // H) ** -0.5
    SCALE1 = 1.0 / (WSCALE * WSCALE)

    with ExitStack() as ctx:
        def sb(name, shape, dt):
            return ctx.enter_context(nc.sbuf_tensor(name, shape, dt))

        def sem(name):
            return ctx.enter_context(nc.semaphore(name))

        proj = ctx.enter_context(nc.psum_tensor("proj", [P, 2, 512], F32))
        mps = ctx.enter_context(nc.psum_tensor("mps", [P, 2, 512], F32))
        sps = ctx.enter_context(nc.psum_tensor("sps", [P, 2, 512], F32))
        ops = ctx.enter_context(nc.psum_tensor("ops", [P, 2, 512], F32))

        ident = sb("ident", [P, P], F32)
        ones = sb("ones", [P, P], F32)
        mask = sb("mask", [P, 4], F32)
        wraw0 = sb("wraw0", [P, 10, C], F32)
        wtmp0 = sb("wtmp0", [P, 4, C], F32)
        wt0 = sb("wt0", [P, 10, C], F16)
        wqd0 = sb("wqd0", [P, KT, 4, P], F16)
        wsum = sb("wsum", [P, 4], F32)
        gam = sb("gam", [P, 4], F32)
        thr = sb("thr", [P, 4], F32)
        nthr = sb("nthr", [P, 4], F32)
        wraw1 = sb("wraw1", [P, 2, 2048], F32)
        wh1 = sb("wh1", [P, 4, 2048], F16)
        wl1 = sb("wl1", [P, 4, 2048], F16)
        bqd = sb("bqd", [P, 4], F32)
        bkp = sb("bkp", [P, KT], F32)
        bvp = sb("bvp", [P, 4], F32)
        bob = sb("bob", [P, C], F32)
        lngp = sb("lngp", [P, KT], F32)
        lnbp = sb("lnbp", [P, KT], F32)
        nwp = sb("nwp", [P, KT], F32)

        ctx32 = sb("ctx32", [P, KT, S], F32)
        ctxh = sb("ctxh", [P, KT, S], F16)
        ctxl = sb("ctxl", [P, KT, S], F16)
        k32 = sb("k32", [P, 5, S], F32)
        KA = [sb("KA0", [P, 4, S], F16), sb("KA1", [P, H, S], F16)]
        KB = [sb("KB0", [P, 4, S], F16), sb("KB1", [P, H, S], F16)]
        qA = [sb("qA0", [P, H, T], F16), sb("qA1", [P, H, T], F16)]
        qB = [sb("qB0", [P, H, T], F16), sb("qB1", [P, H, T], F16)]
        V0 = sb("V0", [P, 3, H, 32], F32)
        V1 = sb("V1", [P, 3, 8, 192], F32)
        x32 = sb("x32", [P, C], F32)
        xb = sb("xb", [P, C], F32)
        x1 = sb("x1", [P, C], F32)
        xout = sb("xout", [P, C], F32)
        stats = [sb(f"stats{l}", [P, 6], F32) for l in range(2)]
        mv = [sb(f"mv{l}", [P, 2], F32) for l in range(2)]
        small = [sb(f"small{l}", [P, 8], F32) for l in range(2)]
        xn = [sb(f"xn{l}", [P, C], F32) for l in range(2)]
        xT32 = [sb(f"xT32_{l}", [P, KT, T], F32) for l in range(2)]
        xTh = [sb(f"xTh{l}", [P, KT, T], F16) for l in range(2)]
        xTl = [sb(f"xTl{l}", [P, KT, T], F16) for l in range(2)]
        q32 = sb("q32", [P, 2, 4, T], F32)
        q32_0 = sb("q32_0", [P, 4, T], F32)
        qh0 = sb("qh0", [P, 4, T], F16)
        ql0 = sb("ql0", [P, 4, T], F16)
        gate = sb("gate", [P, 4], F32)
        mx = [sb(f"mx{l}", [P, H], F32) for l in range(2)]
        mT = [sb(f"mT{l}", [P, T], F16) for l in range(2)]
        prob = sb("prob", [P, 4, G], F32)
        rec0 = sb("rec0", [P, 2, 2 * T], F32)
        rcp0 = sb("rcp0", [P, 2, 2 * T], F32)
        on0 = sb("on0", [P, 4, T], F32)
        o32_0 = sb("o32_0", [P, 4, T], F32)
        oh0 = sb("oh0", [P, 4, T], F16)
        ol0 = sb("ol0", [P, 4, T], F16)
        lns1 = sb("lns1", [P, 2, G], F32)
        rec1 = sb("rec1", [P, 2, G], F32)
        new1 = sb("new1", [P, 2, 2, G], F32)
        o32_1 = sb("o32_1", [P, 8, T], F32)
        oh1 = sb("oh1", [P, 8, T], F16)
        ol1 = sb("ol1", [P, 8, T], F16)

        const_in = sem("const_in")
        w0_in = sem("w0_in")
        w1_in = [sem(f"w1_in{i}") for i in range(2)]
        pad_zero = sem("pad_zero")
        setup_pool = sem("setup_pool")
        setup_ones = sem("setup_ones")
        setup_fill = sem("setup_fill")
        w_sum = sem("w_sum")
        gam_mm = sem("gam_mm")
        gam_ok = sem("gam_ok")
        w_step = sem("w_step")
        w0_ok = sem("w0_ok")
        w1_hi = sem("w1_hi")
        w1_lo = sem("w1_lo")
        proj_full = [sem(f"proj_full{i}") for i in range(2)]
        proj_read = [sem(f"proj_read{i}") for i in range(2)]
        ctx_in = sem("ctx_in")
        ctx_hi = sem("ctx_hi")
        ctx_split = sem("ctx_split")
        k_hi = sem("k_hi")
        k_lo = sem("k_lo")
        kb_in = [sem(f"kb_in{l}") for l in range(2)]
        x_in = sem("x_in")
        xb_ready = sem("xb_ready")
        st_done = [sem(f"st_done{l}") for l in range(2)]
        ag_done = [sem(f"ag_done{l}") for l in range(2)]
        ms_done = sem("ms_done")
        ve_done = [sem(f"ve_done{l}") for l in range(2)]
        ln_done = [sem(f"ln_done{l}") for l in range(2)]
        rs_done = [sem(f"rs_done{l}") for l in range(2)]
        nw_done = [sem(f"nw_done{l}") for l in range(2)]
        xn_ready = [sem(f"xn_ready{l}") for l in range(2)]
        xTh_ready = [sem(f"xTh_ready{l}") for l in range(2)]
        xTl_ready = [sem(f"xTl_ready{l}") for l in range(2)]
        qA1_ready = sem("qA1_ready")
        qB1_ready = sem("qB1_ready")
        qh0_ready = sem("qh0_ready")
        ql0_ready = sem("ql0_ready")
        qA0_ready = sem("qA0_ready")
        q0_ready = sem("q0_ready")
        max_full = sem("max_full")
        max_done = sem("max_done")
        mrow_in = [sem(f"mrow_in{l}") for l in range(2)]
        s_full = sem("s_full")
        exp_done = sem("exp_done")
        prob_used = sem("prob_used")
        o_done = sem("o_done")
        shuf_done = sem("shuf_done")
        rcp0_done = sem("rcp0_done")
        o32_0_ready = sem("o32_0_ready")
        oh0_ready = sem("oh0_ready")
        ol0_ready = sem("ol0_ready")
        lns_done = sem("lns_done")
        rec1_done = sem("rec1_done")
        new1_done = sem("new1_done")
        oh1_ready = sem("oh1_ready")
        ol1_ready = sem("ol1_ready")
        out_stored = sem("out_stored")

        N_CONST_DMA = 2 + 1 + 4 + 3 + 1
        N_W0_DMA = 3 + 4

        block = ctx.enter_context(nc.Block())

        def filled(eng, name, b):
            i, before = turn(name, b, LAST)
            eng.wait_ge(proj_full[i], before + 1)

        def taken(eng, name, b):
            i, before = turn(name, b, LAST)
            eng.wait_ge(proj_read[i], before + 1)

        def place0(s, j):
            return 8 * (s % 2) + 4 * (s // 2) + j

        def heads1(g):
            return [g % 2 + 2 * i for i in range(4 * (g // 2), 4 * (g // 2) + 4)]

        @block.sync
        def _(sp):
            sp.dma_start(ctx32[:], ctxT[0].rearrange("(k p) s -> p k s", p=P)).then_inc(ctx_in, 16)
            sp.dma_start(x32[0:T, :], x[0]).then_inc(x_in, 16)
            for i, w in enumerate((WqT0, WkT0, WvT0)):
                sp.dma_start(wraw0[:, 2 * i:2 * i + 2, :], w.rearrange("(k p) n -> p k n", p=P)).then_inc(w0_in, 16)
            sp.wait_ge(pad_zero, 1)
            wo_heads = WoT0.rearrange("(s j d) n -> j d s n", j=4, d=16)
            for j in range(4):
                sp.dma_start(wraw0[32 * j:32 * j + 16, 6:10, :], wo_heads[j]).then_inc(w0_in, 16)
            for half in range(2):
                sp.dma_start(bqd[64 * half:64 * half + 64, :], bq).then_inc(const_in, 16)
            sp.dma_start(bkp[:], bk).then_inc(const_in, 16)
            for j in range(4):
                sp.dma_start(bvp[32 * j:32 * j + 16, :], bv[j]).then_inc(const_in, 16)
            sp.dma_start(lngp[:], ln_g).then_inc(const_in, 16)
            sp.dma_start(lnbp[:], ln_b).then_inc(const_in, 16)
            sp.dma_start(nwp[:], norm_w).then_inc(const_in, 16)
            sp.dma_start(bob[0:T, :], bo.broadcast_to([T, C])).then_inc(const_in, 16)

            def load_w1(i, w):
                if i >= 2:
                    sp.wait_ge(w1_lo, i - 1)
                sp.dma_start(wraw1[:, i % 2, :].rearrange("p (k n) -> p k n", n=w.shape[1]),
                             w.rearrange("(k p) n -> p k n", p=P)).then_inc(w1_in[i % 2], 16)

            load_w1(0, wk1)
            load_w1(1, wv1)

            def copy_kb(layer, tiles):
                for odd in range(2):
                    r = slice(64 * odd, 64 * odd + 64)
                    sp.dma_start(KB[layer][r, odd:tiles:2, :], KA[layer][r, odd:tiles:2, :]).then_inc(kb_in[layer], 16)

            def load(n):
                sp.wait_ge(ctx_split, n)
                sp.dma_start(ctx32[:], ctxT[n].rearrange("(k p) s -> p k s", p=P)).then_inc(ctx_in, 16)

            def load_x(n):
                sp.wait_ge(xb_ready, n)
                sp.dma_start(x32[0:T, :], x[n]).then_inc(x_in, 16)

            def rows0(n):
                taken(sp, "mT0", n)
                for odd in range(2):
                    r = 0 if odd else 64
                    sp.dma_start(qB[0][r:r + 1, 8 * odd:8 * odd + 8, :], mT[0][8 * odd:8 * odd + 8, :]
                                 ).then_inc(mrow_in[0], 16)

            def rows1(b):
                taken(sp, "mT1", b)
                for odd in range(2):
                    r = 0 if odd else 64
                    sp.dma_start(qB[1][r:r + 1, odd:H:2, :], mT[1][odd:H:2, :]).then_inc(mrow_in[1], 16)

            def store(b):
                taken(sp, "O1", b)
                sp.dma_start(out[b], xout[0:T, :]).then_inc(out_stored, 16)

            def body(b, n, more):
                if more:
                    load(n + 1)
                if n is not None:
                    taken(sp, "K0.1", n)
                    copy_kb(0, 4)
                if b is not None:
                    rows1(b)
                if more:
                    load_x(n + 1)
                if n is not None:
                    rows0(n)
                if b is not None:
                    store(b)
                else:
                    load_w1(2, wq1)
                    load_w1(3, wo1)
                if n is not None:
                    sp.wait_ge(k_hi, n * 8 + 8)
                    copy_kb(1, H)

            sp.wait_ge(setup_fill, 1)
            body(None, 0, True)
            with sp.Fori(0, LAST - 1) as b:
                body(b, b + 1, True)
            body(LAST - 1, LAST, False)
            body(LAST, None, False)
            sp.wait_ge(out_stored, 16 * B + 16)

        @block.tensor
        def _(pe):
            def take(name, b):
                i, before = turn(name, b, LAST)
                pe.wait_ge(proj_read[i], before)
                return proj[:, i, :], proj_full[i]

            bank, full = proj[:, 0, :], gam_mm
            pe.wait_ge(setup_ones, 1)
            pe.wait_ge(w_sum, 4)
            pe.matmul(bank[:, 0:4], ones[:], wsum[:], start=True, stop=True).then_inc(full, 1)

            def key_tile0(t, b):
                bank, full = take(f"K0.{t}", b)
                for n, (k, c) in enumerate((k, c) for k in range(KT) for c in (ctxh, ctxl)):
                    mm = pe.matmul(bank[:, 0:S], wt0[:, 2 + k, P * t:P * t + P], c[:, k, :],
                                   start=n == 0, stop=n == 2 * KT - 1)
                mm.then_inc(full, 1)

            def value_tile0(c, b):
                at, rows = CH[c]
                bank, full = take(f"V0.{c}", b)
                for n, (k, cc) in enumerate((k, cc) for k in range(KT) for cc in (ctxh, ctxl)):
                    mm = pe.matmul(bank[0:rows, 0:C], cc[:, k, at:at + rows], wt0[:, 4 + k, :],
                                   start=n == 0, stop=n == 2 * KT - 1)
                mm.then_inc(full, 1)

            def transpose_x(layer, b):
                bank, full = take(f"xT{layer}", b)
                pe.wait_ge(xn_ready[layer], b + 1)
                for k in range(KT):
                    mm = pe.transpose(bank[:, T * k:T * k + T], xn[layer][0:T, P * k:P * k + P], ident[0:T, 0:T])
                mm.then_inc(full, 1)

            def queries0(b):
                bank, full = take("q0", b)
                pe.wait_ge(xTl_ready[0], b + 1)
                for s in range(4):
                    for n, (k, xx) in enumerate((k, xx) for k in range(KT) for xx in (xTh[0], xTl[0])):
                        mm = pe.matmul(bank[:, T * s:T * s + T], wqd0[:, k, s, :], xx[:, k, :],
                                       start=n == 0, stop=n == 2 * KT - 1)
                mm.then_inc(full, 1)

            def three(k, wi, cols, data_h, data_l):
                h, l = wh1[:, wi, :], wl1[:, wi, :]
                at = 1024 * k
                w = slice(at + cols[0], at + cols[1])
                return [(h[:, w], data_h), (h[:, w], data_l), (l[:, w], data_h)]

            def key_tile1(j, b):
                bank, full = take(f"K1.{j}", b)
                pairs = [p for k in range(KT) for p in three(k, 0, (P * j, P * j + P), ctxh[:, k, :], ctxl[:, k, :])]
                for n, (w, c) in enumerate(pairs):
                    mm = pe.matmul(bank[:, 0:S], w, c, start=n == 0, stop=n == len(pairs) - 1)
                mm.then_inc(full, 1)

            def value_tile1(u, b):
                bank, full = take(f"V1.{u}", b)
                at, rows = CH[u // 2]
                cols = (512 * (u % 2), 512 * (u % 2) + 512)
                pairs = [p for k in range(KT)
                         for p in three(k, 1, cols, ctxh[:, k, at:at + rows], ctxl[:, k, at:at + rows])]
                for n, (w, c) in enumerate(pairs):
                    mm = pe.matmul(bank[0:rows, :], c, w, start=n == 0, stop=n == len(pairs) - 1)
                mm.then_inc(full, 1)

            def queries1(half, b):
                pe.wait_ge(xTl_ready[1], b + 1)
                bank, full = take(f"q1.{half}", b)
                for i in range(4):
                    j = 4 * half + i
                    pairs = [p for k in range(KT)
                             for p in three(k, 2, (P * j, P * j + P), xTh[1][:, k, :], xTl[1][:, k, :])]
                    for n, (w, xx) in enumerate(pairs):
                        mm = pe.matmul(bank[:, T * i:T * i + T], w, xx, start=n == 0, stop=n == len(pairs) - 1)
                mm.then_inc(full, 1)

            def row_scores(layer, h, b):
                n = H * layer + h
                if not isinstance(b, int) or b * 2 * H + n >= 2:
                    pe.wait_ge(max_done, b * 2 * H + n - 1)
                tile = KA[layer][:, h if layer else h // 4, :]
                pe.matmul(mps[0:T, n % 2, 0:S], qA[layer][:, h, :], tile, start=True, stop=True).then_inc(max_full, 1)

            def transpose_max(layer, b):
                bank, full = take(f"mT{layer}", b)
                pe.wait_ge(max_done, b * 2 * H + H * (layer + 1))
                pe.transpose(bank[0:H, 0:T], mx[layer][0:T, :], ident[0:T, 0:T]).then_inc(full, 1)

            def scores(layer, u, b):
                n = 12 * layer + u
                g, c = u // 3, u % 3
                at, rows = CH[c]
                if u >= 2:
                    pe.wait_ge(exp_done, b * 24 + n - 1)
                if layer == 0:
                    pe.matmul(sps[0:rows, n % 2, 0:G], KA[0][:, g, at:at + rows],
                              qA[0][:, 4 * g:4 * g + 4, :], start=True, stop=False)
                    mm = pe.matmul(sps[0:rows, n % 2, 0:G], KB[0][:, g, at:at + rows],
                                   qB[0][:, place0(g, 0):place0(g, 3) + 1, :], start=False, stop=True)
                else:
                    for i, h in enumerate(heads1(g)):
                        o = sps[0:rows, n % 2, T * i:T * i + T]
                        pe.matmul(o, KA[1][:, h, at:at + rows], qA[1][:, h, :], start=True, stop=False)
                        mm = pe.matmul(o, KB[1][:, h, at:at + rows], qB[1][:, h, :], start=False, stop=True)
                mm.then_inc(s_full, 1)

            def weigh(layer, u, b):
                n = 12 * layer + u
                g, c = u // 3, u % 3
                rows = CH[c][1]
                pe.wait_ge(exp_done, b * 24 + n + 1)
                p = prob[0:rows, n % 4, :]
                if c == 0 and (layer == 1 or g % 2 == 0) and (layer == 1 or not isinstance(b, int) or b > 0):
                    pe.wait_ge(o_done, b * 6 + (g + 1 if layer else g // 2 - 1))
                if layer == 0:
                    for j in range(4):
                        mm = pe.matmul(ops[32 * j:32 * j + 32, g // 2, T * (g % 2):T * (g % 2) + T],
                                       V0[0:rows, c, 4 * g + j, :], p[:, T * j:T * j + T],
                                       start=c == 0, stop=c == 2, tile_position=(0, 32 * j))
                else:
                    for i, h in enumerate(heads1(g)):
                        w = V1[0:rows, c, h // 2, 64 * (h % 2):64 * (h % 2) + P]
                        mm = pe.matmul(ops[:, g % 2, T * i:T * i + T], w, p[:, T * i:T * i + T],
                                       start=c == 0 and i == 0, stop=c == 2, skip_group_check=True)
                mm.then_inc(prob_used, 1)

            def project_out(layer, b):
                bank, full = take(f"O{layer}", b)
                if layer == 0:
                    pe.wait_ge(ol0_ready, b * 2 + 2)
                    for n, (s, oo) in enumerate((s, oo) for s in range(4) for oo in (oh0, ol0)):
                        mm = pe.matmul(bank[0:T, 0:C], oo[:, s, :], wt0[:, 6 + s, :], start=n == 0, stop=n == 7)
                else:
                    pe.wait_ge(ol1_ready, b * 4 + 4)
                    for k in range(8):
                        w = slice(C * k, C * k + C)
                        for n, (oo, ww) in enumerate(((oh1, wh1), (oh1, wl1), (ol1, wh1))):
                            mm = pe.matmul(bank[0:T, 0:C], oo[:, k, :], ww[:, 3, w],
                                           start=k == 0 and n == 0, stop=k == 7 and n == 2)
                mm.then_inc(full, 1)

            def body(b, n, more):
                if b is not None:
                    pe.wait_ge(k_lo, b * 20 + 20)
                    pe.wait_ge(qA1_ready, b * 2 + 2)
                    for h in range(8):
                        row_scores(1, h, b)
                if n is not None:
                    pe.wait_ge(ctx_split, n + 1)
                    key_tile0(0, n)
                    key_tile0(1, n)
                for c in range(3):
                    if b is not None:
                        for h in range(8 + 3 * c, min(11 + 3 * c, H)):
                            row_scores(1, h, b)
                    if n is not None:
                        value_tile0(c, n)
                if b is not None:
                    transpose_max(1, b)
                if n is not None:
                    pe.wait_ge(k_lo, n * 20 + 4)
                    pe.wait_ge(qA0_ready, n + 1)
                    for h in range(6 if b is not None else H):
                        row_scores(0, h, n)
                if b is not None:
                    pe.wait_ge(mrow_in[1], b * 32 + 32)
                    pe.wait_ge(qB1_ready, b * 4 + 4)
                    pe.wait_ge(kb_in[1], b * 32 + 32)
                    scores(1, 0, b)
                    scores(1, 1, b)
                    rows = (3, 3, 2, 2)
                    for u in range(12):
                        weigh(1, u, b)
                        if n is not None and u < 4:
                            for h in range(6 + sum(rows[:u]), 6 + sum(rows[:u + 1])):
                                row_scores(0, h, n)
                        if u < 10:
                            scores(1, u + 2, b)
                        if n is not None and u == 6:
                            transpose_max(0, n)
                elif n is not None:
                    transpose_max(0, n)
                if more:
                    transpose_x(0, n + 1)
                if n is not None:
                    pe.wait_ge(mrow_in[0], n * 32 + 32)
                    pe.wait_ge(q0_ready, n + 1)
                    pe.wait_ge(kb_in[0], n * 32 + 32)
                    scores(0, 0, n)
                    scores(0, 1, n)
                    for u in range(12):
                        weigh(0, u, n)
                        if u < 10:
                            scores(0, u + 2, n)
                        if u == 3 and more:
                            queries0(n + 1)
                        if u == 4 and b is not None:
                            project_out(1, b)
                elif b is not None:
                    project_out(1, b)
                if n is not None:
                    if b is None:
                        pe.wait_ge(w1_lo, 1)
                    for j in range(6):
                        key_tile1(j, n)
                    project_out(0, n)
                    for j in range(6, 8):
                        key_tile1(j, n)
                    if b is None:
                        pe.wait_ge(w1_lo, 2)
                    value_tile1(0, n)
                    transpose_x(1, n)
                    for u in range(1, 4):
                        value_tile1(u, n)
                    if b is None:
                        pe.wait_ge(w1_lo, 3)
                    queries1(0, n)
                    queries1(1, n)
                    value_tile1(4, n)
                    value_tile1(5, n)

            pe.wait_ge(w0_ok, 1)
            pe.wait_ge(setup_pool, 7)
            transpose_x(0, 0)
            queries0(0)
            pe.wait_ge(setup_fill, 1)
            body(None, 0, True)
            with pe.Fori(0, LAST - 1) as b:
                body(b, b + 1, True)
            body(LAST - 1, LAST, False)
            body(LAST, None, False)

        @block.scalar
        def _(act):
            def full(name, b):
                i, before = turn(name, b, LAST)
                act.wait_ge(proj_full[i], before + 1)
                return proj[:, i, :], proj_read[i]

            def key_tile(layer, t, scale, bias, b):
                bank, free = full(f"K{layer}.{t}", b)
                n = 2 * layer + t
                if not isinstance(b, int) or b * 10 + n >= 5:
                    act.wait_ge(k_lo, b * 20 + 2 * (n - 4))
                slot = k32[:, n % 5, :]
                if layer == 0:
                    for half in range(2):
                        r = slice(64 * half, 64 * half + 64)
                        nc.scalar.activation(KA[0][r, 2 * t + half, :], bank[r, 0:S], ACT.Identity,
                                             scale=scale[r, :], bias=bias[r, :])
                nc.scalar.activation(slot, bank[:, 0:S], ACT.Identity, scale=scale, bias=bias
                                     ).then_inc(free, 1)

            def values0(c, b):
                bank, free = full(f"V0.{c}", b)
                rows = CH[c][1]
                nc.scalar.activation(V0[0:rows, c, :, 0:16], bank[0:rows, 0:C].rearrange("p (h d) -> p h d", d=16),
                                     ACT.Copy).then_inc(free, 1)

            def values1(u, b):
                bank, free = full(f"V1.{u}", b)
                rows = CH[u // 2][1]
                at = 4 * (u % 2)
                dst = V1[0:rows, u // 2, at:at + 4, :].rearrange("p j (w d) -> p j w d", d=64)[:, :, 0:3:2, :]
                src = bank[0:rows, :].rearrange("p (j w d) -> p j w d", w=2, d=64)
                nc.scalar.activation(dst, src, ACT.Copy).then_inc(free, 1)

            def row_max(layer, b):
                bank, free = full(f"mT{layer}", b)
                nc.scalar.activation(mT[layer][0:H, :], bank[0:H, 0:T], ACT.Copy, scale=-1.0 / MROW
                                     ).then_inc(free, 1)

            def rsqrt(layer, nb):
                act.wait_ge(ve_done[layer], nb + 1)
                s = small[layer]
                nc.scalar.activation(s[0:T, 1:2], s[0:T, 0:1], ACT.Ln).then_inc(ln_done[layer], 1)
                act.wait_ge(ln_done[layer], nb + 1)
                nc.scalar.activation(s[0:T, 2:3], s[0:T, 1:2], ACT.Exp, scale=-0.5).then_inc(rs_done[layer], 1)

            def transposed_x(layer, b):
                bank, free = full(f"xT{layer}", b)
                if layer == 0:
                    for k in range(KT):
                        i = nc.scalar.activation(xT32[0][:, k, :], bank[:, T * k:T * k + T], ACT.Identity,
                                                 scale=lngp[:, k:k + 1], bias=lnbp[:, k:k + 1])
                else:
                    for k in range(KT):
                        i = nc.scalar.activation(xT32[1][:, k, :], bank[:, T * k:T * k + T], ACT.Identity,
                                                 scale=nwp[:, k:k + 1])
                i.then_inc(free, 1)

            def queries0(b):
                bank, free = full("q0", b)
                for s in range(4):
                    i = nc.scalar.activation(q32_0[:, s, :], bank[:, T * s:T * s + T], ACT.Identity,
                                             scale=gam[:, 0:1], bias=bqd[:, s:s + 1])
                i.then_inc(free, 1)

            def queries1(half, b):
                bank, free = full(f"q1.{half}", b)
                nc.scalar.activation(q32[:, half, :, :], bank[:, 0:G].rearrange("p (j t) -> p j t", t=T),
                                     ACT.Copy).then_inc(free, 1)

            def exp(layer, u, b):
                n = 12 * layer + u
                rows = CH[u % 3][1]
                act.wait_ge(s_full, b * 24 + n + 1)
                if u >= 4:
                    act.wait_ge(prob_used, b * 24 + n - 3)
                nc.scalar.activation(prob[0:rows, n % 4, :], sps[0:rows, n % 2, 0:G], ACT.Exp,
                                     scale=SCALE1 if layer else SCALE0).then_inc(exp_done, 1)

            def reciprocal1(g, b):
                act.wait_ge(prob_used, b * 24 + 12 + 3 * g + 3)
                odd = g % 2
                r = slice(64 * odd, 64 * odd + 64)
                den = slice(64 - 64 * odd, P - 64 * odd)
                nc.scalar.activation(lns1[r, odd, :], ops[den, odd, 0:G], ACT.Ln).then_inc(lns_done, 1)
                act.wait_ge(lns_done, b * 4 + g + 1)
                nc.scalar.activation(rec1[r, odd, :], lns1[r, odd, :], ACT.Exp, scale=-1.0).then_inc(rec1_done, 1)

            def output0(i, n):
                act.wait_ge(o_done, n * 6 + i + 1)
                for s in range(2 * i, 2 * i + 2):
                    ins = nc.scalar.activation(o32_0[:, s, :], on0[:, s, :], ACT.Identity,
                                               scale=gam[:, 2:3], bias=bvp[:, s:s + 1])
                ins.then_inc(o32_0_ready, 1)

            def split_ctx_hi(n):
                act.wait_ge(ctx_in, n * 16 + 16)
                nc.scalar.activation(ctxh[:], ctx32[:], ACT.Copy).then_inc(ctx_hi, 1)

            def w1_part(i):
                act.wait_ge(w1_in[i % 2], 16 * (i // 2 + 1))
                nc.scalar.activation(wh1[:, i, :], wraw1[:, i % 2, :], ACT.Copy, scale=WSCALE).then_inc(w1_hi, 1)

            def body(b, n, more):
                if n is not None:
                    split_ctx_hi(n)
                    key_tile(0, 0, gam[:, 1:2], bkp[:, 0:1], n)
                    key_tile(0, 1, gam[:, 1:2], bkp[:, 1:2], n)
                    for c in range(3):
                        values0(c, n)
                if b is not None:
                    row_max(1, b)
                    for u in range(12):
                        exp(1, u, b)
                        if u % 3 == 1 and u > 3:
                            reciprocal1(u // 3 - 1, b)
                        if u == 8 and n is not None:
                            row_max(0, n)
                        if u == 9 and more:
                            rsqrt(0, n + 1)
                    reciprocal1(3, b)
                else:
                    w1_part(0)
                    w1_part(1)
                    row_max(0, n)
                    rsqrt(0, n + 1)
                if more:
                    transposed_x(0, n + 1)
                if n is not None:
                    for u in range(12):
                        exp(0, u, n)
                        if u == 5 and more:
                            queries0(n + 1)
                        if u == 9:
                            output0(0, n)
                    if b is None:
                        w1_part(2)
                    for j in range(3):
                        key_tile(1, j, 1.0, 0.0, n)
                    output0(1, n)
                    for j in range(3, 8):
                        key_tile(1, j, 1.0, 0.0, n)
                    rsqrt(1, n)
                    values1(0, n)
                    transposed_x(1, n)
                    for u in range(1, 4):
                        values1(u, n)
                    queries1(0, n)
                    queries1(1, n)
                    if b is None:
                        w1_part(3)
                    values1(4, n)
                    values1(5, n)

            nc.scalar.preload_act_table_set("natural_log_exp_and_others")
            act.wait_ge(const_in, 16 * N_CONST_DMA)
            rsqrt(0, 0)
            transposed_x(0, 0)
            act.wait_ge(gam_ok, 1)
            queries0(0)
            body(None, 0, True)
            with act.Fori(0, LAST - 1) as b:
                body(b, b + 1, True)
            body(LAST - 1, LAST, False)
            body(LAST, None, False)

        @block.vector
        def _(dve):
            steps = [0]

            def step(ins):
                steps[0] += 1
                ins.then_inc(w_step, 1)
                dve.wait_ge(w_step, steps[0])

            def key_tile1(t, b):
                taken(dve, f"K1.{t}", b)
                slot = (2 + t) % 5
                nc.vector.tensor_copy(KA[1][0:64, 2 * t, :], k32[0:64, slot, :])
                nc.vector.tensor_copy(KA[1][64:P, 2 * t + 1, :], k32[64:P, slot, :]).then_inc(k_hi, 1)

            def statistics(layer, nb):
                src = x1 if layer else x32
                nc.vector.bn_stats(out=stats[layer][0:T, :], in_=src[0:T, :]).then_inc(st_done[layer], 1)
                dve.wait_ge(st_done[layer], nb + 1)
                nc.vector.memset(gate[0:1, layer:layer + 1], 0.0)
                m = mv[layer]
                nc.vector.bn_aggr(out=m[0:T, :], in_=stats[layer][0:T, :]).then_inc(ag_done[layer], 1)
                dve.wait_ge(ag_done[layer], nb + 1)
                s = small[layer]
                var = m[0:T, 1:2]
                if layer:
                    nc.vector.scalar_tensor_tensor(out=s[0:T, 3:4], in0=m[0:T, 0:1], scalar=m[0:T, 0:1],
                                                   in1=m[0:T, 1:2], op0=ALU.mult, op1=ALU.add).then_inc(ms_done, 1)
                    dve.wait_ge(ms_done, nb + 1)
                    var = s[0:T, 3:4]
                nc.vector.tensor_scalar(s[0:T, 0:1], var, RMS_EPS if layer else LN_EPS, None, ALU.add
                                        ).then_inc(ve_done[layer], 1)

            def normalise_x(layer, nb):
                s, n = small[layer], nw_done[layer]
                y = s[0:T, 2:3]
                dve.wait_ge(rs_done[layer], nb + 1)
                nc.vector.tensor_tensor(s[0:T, 4:5], y, y, ALU.mult).then_inc(n, 1)
                dve.wait_ge(n, nb * 3 + 1)
                nc.vector.tensor_scalar(s[0:T, 5:6], s[0:T, 4:5], s[0:T, 0:1], -0.5, ALU.mult, ALU.mult).then_inc(n, 1)
                dve.wait_ge(n, nb * 3 + 2)
                nc.vector.tensor_scalar(s[0:T, 6:7], s[0:T, 5:6], 1.5, y, ALU.add, ALU.mult).then_inc(n, 1)
                dve.wait_ge(n, nb * 3 + 3)
                if layer:
                    i = nc.vector.tensor_scalar(xn[1][0:T, :], x1[0:T, :], s[0:T, 6:7], None, ALU.mult)
                else:
                    i = nc.vector.tensor_scalar(xn[0][0:T, :], x32[0:T, :], mv[0][0:T, 0:1], s[0:T, 6:7],
                                                ALU.subtract, ALU.mult)
                i.then_inc(xn_ready[layer], 1)

            def x_hi(layer, b):
                taken(dve, f"xT{layer}", b)
                nc.vector.tensor_copy(xTh[layer][:], xT32[layer][:]).then_inc(xTh_ready[layer], 1)

            def queries0_hi(nb):
                taken(dve, "q0", nb)
                nc.vector.tensor_copy(qh0[:], q32_0[:]).then_inc(qh0_ready, 1)

            def mask_queries0_hi(nb):
                dve.wait_ge(qh0_ready, nb + 1)
                for j in range(4):
                    i = nc.vector.tensor_scalar(qA[0][:, j:H:4, :], qh0[:], mask[:, j:j + 1], None, ALU.mult)
                i.then_inc(qA0_ready, 1)

            def mask_queries0_lo(nb):
                dve.wait_ge(ql0_ready, nb + 1)
                for j in range(4):
                    for odd in range(2):
                        r = slice(64 * odd, 64 * odd + 64)
                        i = nc.vector.tensor_scalar(qB[0][r, 8 * odd + j:8 * odd + 8:4, :], ql0[r, odd:4:2, :],
                                                    mask[r, j:j + 1], None, ALU.mult)
                i.then_inc(q0_ready, 1)

            def queries1_hi(half, b):
                taken(dve, f"q1.{half}", b)
                for odd in range(2):
                    r = slice(64 * odd, 64 * odd + 64)
                    for to in range(2):
                        i = nc.vector.tensor_copy(qA[1][64 * to:64 * to + 64, 8 * half + odd:8 * half + 8:2, :],
                                                  q32[r, half, :, :])
                i.then_inc(qA1_ready, 1)

            def row_max(layer, h, b):
                n = H * layer + h
                dve.wait_ge(max_full, b * 2 * H + n + 1)
                at = h if layer else place0(h // 4, h % 4)
                nc.vector.tensor_reduce(mx[layer][0:T, at:at + 1], mps[0:T, n % 2, 0:S], AX.X, ALU.max
                                        ).then_inc(max_done, 1)

            def normalise0(i, b):
                dve.wait_ge(prob_used, b * 24 + 6 * i + 6)
                nc.vector.memset(gate[0:1, 2 + i:3 + i], 0.0)
                src = ops[:, i, 0:2 * T]
                nc.vector.stream_shuffle(rec0[:, i, :], src, list(range(16, 32)) * 2).then_inc(shuf_done, 1)
                dve.wait_ge(shuf_done, b * 2 + i + 1)
                nc.vector.reciprocal(rcp0[:, i, :], rec0[:, i, :]).then_inc(rcp0_done, 1)
                dve.wait_ge(rcp0_done, b * 2 + i + 1)
                nc.vector.tensor_tensor(on0[:, 2 * i:2 * i + 2, :], src.rearrange("p (s t) -> p s t", t=T),
                                        rcp0[:, i, :].rearrange("p (s t) -> p s t", t=T), ALU.mult).then_inc(o_done, 1)

            def normalise1(g, b):
                odd = g % 2
                r = slice(64 * odd, 64 * odd + 64)
                den = slice(64 - 64 * odd, P - 64 * odd)
                at = 4 * (g // 2)
                dve.wait_ge(rec1_done, b * 4 + g + 1)
                nc.vector.tensor_tensor(new1[r, odd, 0, :], ops[den, odd, 0:G], rec1[r, odd, :], ALU.mult
                                        ).then_inc(new1_done, 1)
                dve.wait_ge(new1_done, b * 8 + 2 * g + 1)
                nc.vector.scalar_tensor_tensor(out=new1[r, odd, 1, :], in0=new1[r, odd, 0, :], scalar=2.0,
                                               in1=rec1[r, odd, :], op0=ALU.subtract, op1=ALU.mult
                                               ).then_inc(new1_done, 1)
                dve.wait_ge(new1_done, b * 8 + 2 * g + 2)
                nc.vector.scalar_tensor_tensor(out=o32_1[r, at:at + 4, :],
                                               in0=ops[r, odd, 0:G].rearrange("p (j t) -> p j t", t=T), scalar=-1.0,
                                               in1=new1[r, odd, 1, :].rearrange("p (j t) -> p j t", t=T),
                                               op0=ALU.mult, op1=ALU.mult).then_inc(o_done, 1)
                dve.wait_ge(o_done, b * 6 + 2 + g + 1)
                nc.vector.tensor_copy(oh1[r, at:at + 4, :], o32_1[r, at:at + 4, :]).then_inc(oh1_ready, 1)

            step(nc.vector.memset(wraw0[:, 6:10, :], 0.0))
            nc.vector.memset(bvp[:], 0.0).then_inc(pad_zero, 1)
            nc.vector.memset(gate[:], 0.0).then_inc(out_stored, 16)
            nc.vector.memset(ones[:], 1.0).then_inc(setup_ones, 1)
            dve.wait_ge(w0_in, 16 * N_W0_DMA)
            for i, (a, z) in enumerate(((0, 2), (2, 4), (4, 6), (6, 10))):
                nc.vector.tensor_reduce(wsum[:, i:i + 1], wraw0[:, a:z, :], AX.XY, ALU.add,
                                        apply_absolute_value=True).then_inc(w_sum, 1)
            dve.wait_ge(gam_mm, 1)
            step(nc.vector.tensor_scalar(gam[:], proj[:, 0, 0:4], 1.0 / (C * C), None, ALU.mult))
            step(nc.vector.tensor_scalar(thr[:], gam[:], Q_EPS, 0.5, ALU.add, ALU.mult))
            nc.vector.tensor_scalar(nthr[:], thr[:], -1.0, None, ALU.mult).then_inc(gam_ok, 1)
            dve.wait_ge(gam_ok, 1)
            for i, (a, z) in enumerate(((0, 2), (2, 4), (4, 6), (6, 10))):
                step(nc.vector.tensor_scalar(wtmp0[:, 0:z - a, :], wraw0[:, a:z, :], nthr[:, i:i + 1], None, ALU.is_lt))
                step(nc.vector.scalar_tensor_tensor(out=wt0[:, a:z, :], in0=wraw0[:, a:z, :], scalar=thr[:, i:i + 1],
                                                    in1=wtmp0[:, 0:z - a, :], op0=ALU.is_gt, op1=ALU.subtract))
            for k in range(KT):
                for half in range(2):
                    i = nc.vector.tensor_copy(wqd0[:, k, :, 64 * half:64 * half + 64],
                                              wt0[:, k, :].rearrange("p (s d) -> p s d", d=64))
            i.then_inc(w0_ok, 1)
            for layer in range(2):
                nc.vector.memset(KB[layer][:], 0.0)
                step(nc.vector.memset(qB[layer][:], 0.0))
                nc.vector.memset(KB[layer][64:65, 0::2, :], MROW)
                nc.vector.memset(KB[layer][0:1, 1::2, :], MROW)
            nc.vector.memset(V0[:, :, :, 16:32], 1.0)
            nc.vector.memset(V1[:, :, :, 64:P], 1.0).then_inc(setup_fill, 1)
            dve.wait_ge(x_in, 16)
            statistics(0, 0)
            normalise_x(0, 0)
            x_hi(0, 0)
            queries0_hi(0)
            mask_queries0_hi(0)
            mask_queries0_lo(0)

            def first_residual(n):
                filled(dve, "O0", n)
                dve.wait_ge(xb_ready, n + 1)
                i, _ = turn("O0", n, LAST)
                nc.vector.scalar_tensor_tensor(out=x1[0:T, :], in0=proj[0:T, i, 0:C], scalar=gam[0:T, 3:4],
                                               in1=xb[0:T, :], op0=ALU.mult, op1=ALU.add).then_inc(proj_read[i], 1)
                taken(dve, "O0", n)

            def second_residual(b):
                filled(dve, "O1", b)
                dve.wait_ge(out_stored, b * 16 + 16)
                i, _ = turn("O1", b, LAST)
                nc.vector.scalar_tensor_tensor(out=xout[0:T, :], in0=proj[0:T, i, 0:C], scalar=SCALE1,
                                               in1=x1[0:T, :], op0=ALU.mult, op1=ALU.add).then_inc(proj_read[i], 1)

            def maxima(layer, heads, b):
                if b is not None:
                    for h in heads:
                        row_max(layer, h, b)

            def output0_hi(i, n):
                dve.wait_ge(o32_0_ready, n * 2 + i + 1)
                nc.vector.tensor_copy(oh0[:, 2 * i:2 * i + 2, :], o32_0[:, 2 * i:2 * i + 2, :]).then_inc(oh0_ready, 1)

            def w1_part(i):
                dve.wait_ge(w1_hi, i + 1)
                nc.vector.scalar_tensor_tensor(out=wl1[:, i, :], in0=wraw1[:, i % 2, :], scalar=WSCALE,
                                               in1=wh1[:, i, :], op0=ALU.mult, op1=ALU.subtract).then_inc(w1_lo, 1)

            def body(b, n, more):
                maxima(1, range(H), b)
                if n is not None:
                    maxima(0, range(H), n)
                if b is not None:
                    normalise1(0, b)
                    normalise1(1, b)
                if more:
                    dve.wait_ge(x_in, n * 16 + 32)
                    statistics(0, n + 1)
                if b is not None:
                    normalise1(2, b)
                if more:
                    normalise_x(0, n + 1)
                if b is not None:
                    normalise1(3, b)
                if more:
                    x_hi(0, n + 1)
                    queries0_hi(n + 1)
                if b is not None:
                    second_residual(b)
                else:
                    w1_part(0)
                    w1_part(1)
                if n is not None:
                    normalise0(0, n)
                    output0_hi(0, n)
                    normalise0(1, n)
                    if b is None:
                        w1_part(2)
                    key_tile1(0, n)
                    key_tile1(1, n)
                    output0_hi(1, n)
                    for j in range(2, 6):
                        key_tile1(j, n)
                    first_residual(n)
                    statistics(1, n)
                    key_tile1(6, n)
                    normalise_x(1, n)
                    key_tile1(7, n)
                    x_hi(1, n)
                    if more:
                        mask_queries0_hi(n + 1)
                        mask_queries0_lo(n + 1)
                    queries1_hi(0, n)
                    queries1_hi(1, n)
                    if b is None:
                        w1_part(3)

            body(None, 0, True)
            with dve.Fori(0, LAST - 1) as b:
                body(b, b + 1, True)
            body(LAST - 1, LAST, False)
            body(LAST, None, False)

        @block.gpsimd
        def _(pool):
            def setup(ins, n):
                ins.then_inc(setup_pool, 1)
                pool.wait_ge(setup_pool, n)

            setup(nc.gpsimd.memset(ident[:], 0.0), 1)
            setup(nc.gpsimd.memset(mask[:], 1.0), 2)
            setup(nc.gpsimd.affine_select(out=ident[:], in_=ident[:], compare_op=ALU.not_equal, fill=1.0, base=0,
                                          pattern=[[-1, P]], channel_multiplier=1), 3)
            for half in range(2):
                m = mask[64 * half:64 * half + 64, :]
                setup(nc.gpsimd.affine_select(out=m, in_=m, compare_op=ALU.is_ge, fill=0.0, base=0,
                                              pattern=[[-16, 4]], channel_multiplier=1), 4 + 2 * half)
                setup(nc.gpsimd.affine_select(out=m, in_=m, compare_op=ALU.is_ge, fill=0.0, base=15,
                                              pattern=[[16, 4]], channel_multiplier=-1), 5 + 2 * half)

            def lo_part(out, a, hi, done, count):
                nc.gpsimd.tensor_tensor(out, a, hi, ALU.subtract).then_inc(done, 1)
                pool.wait_ge(done, count)

            def split_ctx_lo(nb):
                pool.wait_ge(ctx_hi, nb + 1)
                lo_part(ctxl[:], ctx32[:], ctxh[:], ctx_split, nb + 1)

            def key_tile(layer, t, b):
                if layer:
                    pool.wait_ge(k_hi, b * 8 + t + 1)
                else:
                    taken(pool, f"K0.{t}", b)
                n = b * 10 + 2 * layer + t
                slot = k32[:, (2 * layer + t) % 5, :]
                k = KA[layer]
                lo_part(k[64:P, 2 * t, :], slot[0:64, :], k[0:64, 2 * t, :], k_lo, n * 2 + 1)
                lo_part(k[0:64, 2 * t + 1, :], slot[64:P, :], k[64:P, 2 * t + 1, :], k_lo, n * 2 + 2)

            def x_lo(layer, nb):
                pool.wait_ge(xTh_ready[layer], nb + 1)
                lo_part(xTl[layer][:], xT32[layer][:], xTh[layer][:], xTl_ready[layer], nb + 1)

            def queries0_lo(nb):
                pool.wait_ge(qh0_ready, nb + 1)
                lo_part(ql0[:], q32_0[:], qh0[:], ql0_ready, nb + 1)

            def output0_lo(i, n):
                two = slice(2 * i, 2 * i + 2)
                pool.wait_ge(oh0_ready, n * 2 + i + 1)
                lo_part(ol0[:, two, :], o32_0[:, two, :], oh0[:, two, :], ol0_ready, n * 2 + i + 1)

            def queries1_lo(half, nb):
                pool.wait_ge(qA1_ready, nb * 2 + half + 1)
                for odd in range(2):
                    r = slice(64 * odd, 64 * odd + 64)
                    heads = slice(8 * half + odd, 8 * half + 8, 2)
                    lo_part(qB[1][r, heads, :], q32[r, half, :, :], qA[1][r, heads, :],
                            qB1_ready, nb * 4 + 2 * half + odd + 1)

            def body(b, n, more):
                if n is not None:
                    split_ctx_lo(n)
                if b is not None:
                    queries1_lo(0, b)
                if n is not None:
                    key_tile(0, 0, n)
                    key_tile(0, 1, n)
                if b is not None:
                    queries1_lo(1, b)
                if n is not None:
                    pool.wait_ge(x_in, n * 16 + 16)
                    nc.gpsimd.tensor_tensor(xb[0:T, :], x32[0:T, :], bob[0:T, :], ALU.add).then_inc(xb_ready, 1)
                    pool.wait_ge(xb_ready, n + 1)
                if b is not None:
                    for g in range(4):
                        pool.wait_ge(oh1_ready, b * 4 + g + 1)
                        r = slice(64 * (g % 2), 64 * (g % 2) + 64)
                        at = 4 * (g // 2)
                        lo_part(ol1[r, at:at + 4, :], o32_1[r, at:at + 4, :], oh1[r, at:at + 4, :],
                                ol1_ready, b * 4 + g + 1)
                if more:
                    x_lo(0, n + 1)
                    queries0_lo(n + 1)
                if n is not None:
                    output0_lo(0, n)
                    key_tile(1, 0, n)
                    output0_lo(1, n)
                    for j in range(1, 5):
                        key_tile(1, j, n)
                    x_lo(1, n)
                    for j in range(5, 8):
                        key_tile(1, j, n)

            x_lo(0, 0)
            queries0_lo(0)
            pool.wait_ge(const_in, 16 * N_CONST_DMA)
            body(None, 0, True)
            with pool.Fori(0, LAST - 1) as b:
                body(b, b + 1, True)
            body(LAST - 1, LAST, False)
            body(LAST, None, False)


def kernel(x, ctx_1024, L0_xattn_Wq, L0_xattn_bq, L0_xattn_Wk, L0_xattn_bk, L0_xattn_Wv, L0_xattn_bv, L0_xattn_Wo,
           L0_xattn_bo, L0_xattn_ln_gamma, L0_xattn_ln_beta, L1_xattn_wq, L1_xattn_wk, L1_xattn_wv, L1_xattn_wo,
           L1_xattn_norm_w):
    import numpy as np
    import concourse.bacc as bacc
    from concourse.bass_utils import run_bass_kernel_spmd

    def by_partition(v):
        return np.asarray(v).reshape(2, P).T

    laid = {
        "x": x, "ctxT": np.asarray(ctx_1024).transpose(0, 2, 1),
        "WqT0": np.asarray(L0_xattn_Wq).T, "bq": np.asarray(L0_xattn_bq).reshape(4, 64).T,
        "WkT0": np.asarray(L0_xattn_Wk).T, "bk": by_partition(L0_xattn_bk),
        "WvT0": np.asarray(L0_xattn_Wv).T, "bv": np.asarray(L0_xattn_bv).reshape(4, 4, 16).transpose(1, 2, 0),
        "WoT0": np.asarray(L0_xattn_Wo).T, "bo": np.asarray(L0_xattn_bo).reshape(1, -1),
        "ln_g": by_partition(L0_xattn_ln_gamma), "ln_b": by_partition(L0_xattn_ln_beta),
        "wq1": L1_xattn_wq, "wk1": L1_xattn_wk, "wv1": L1_xattn_wv, "wo1": L1_xattn_wo,
        "norm_w": by_partition(L1_xattn_norm_w),
    }
    nc = bacc.Bacc("TRN2", target_bir_lowering=False, num_devices=1)
    arrays, args = {}, []
    for name, a in laid.items():
        a = np.ascontiguousarray(a)
        arrays[f"in_{name}"] = a
        args.append(nc.dram_tensor(f"in_{name}", a.shape, mybir.dt.from_np(a.dtype), kind="ExternalInput").ap())
    y = nc.dram_tensor("out_0", tuple(laid["x"].shape), F32, kind="ExternalOutput").ap()
    build(nc, *args, y)
    r = run_bass_kernel_spmd(nc, [arrays], core_ids=[0])
    return r.results[0]["out_0"]
```

```python
from contextlib import ExitStack

import concourse.bass as bass
from concourse import mybir

ALU = mybir.AluOpType
ACT = mybir.ActivationFunctionType
AX = mybir.AxisListType
F32 = mybir.dt.float32
F16 = mybir.dt.float16

P = 128
WSCALE = 64.0
MROW = 1024.0
LN_EPS = 1e-5
Q_EPS = 1e-5
RMS_EPS = 1e-6

LAYER1 = ("mT1", "V1.4", "V1.5", "oT0", "oT1", "O1")
AHEAD = ("xT0", "q0", "V0.0", "K0.0", "K0.1", "V0.1", "V0.2", "mT0")
BODY_TURNS = (
    ["mT1", "xT0", "V1.4", "V1.5"]
    + ["q0", "V0.0", "K0.0", "O0", "K0.1", "V0.1", "xT1", "oT0", "V0.2"]
    + ["q1.0", "oT1", "K1.0", "q1.1", "K1.1", "K1.2", "O1"] + [f"K1.{j}" for j in range(3, 8)]
    + ["V1.0", "mT0", "V1.1", "V1.2", "V1.3"]
)
FIRST_TURNS = [t for t in BODY_TURNS if t not in LAYER1]
NEAR_LAST_TURNS = [t for t in BODY_TURNS if t not in AHEAD]
assert [t for t in BODY_TURNS if t in AHEAD] == list(AHEAD)
assert all(len(t) % 2 == 0 for t in (LAYER1, AHEAD, BODY_TURNS))


def turn(name, batch, last):
    iteration = batch + (1 if name in LAYER1 else -1 if name in AHEAD else 0)
    start = (len(AHEAD) + len(FIRST_TURNS)) // 2 + (iteration - 1) * (len(BODY_TURNS) // 2)
    turns = BODY_TURNS
    if isinstance(iteration, int):
        if iteration < 0:
            turns, start = AHEAD, 0
        elif iteration == 0:
            turns, start = FIRST_TURNS, len(AHEAD) // 2
        elif iteration == last:
            turns = NEAR_LAST_TURNS
        elif iteration > last:
            turns, start = LAYER1, start - (len(BODY_TURNS) - len(NEAR_LAST_TURNS)) // 2
    n = turns.index(name)
    return n % 2, start + n // 2


def build(nc, x, ctxT, WqT0, bq, WkT0, bk, WvT0, bv, WoT0, bo, ln_g, ln_b, wq1, wk1, wv1, wo1, norm_w, out):
    B, T, C = x.shape
    S = ctxT.shape[2]
    H = 16
    D1 = wq1.shape[1] // H
    assert C == 2 * P and D1 == 64 and T <= P and 2 * P < S <= 3 * P
    KT = C // P
    CH = [(c * P, min(P, S - c * P)) for c in range(3)]
    G = 4 * T
    LAST = B - 1
    SCALE0 = float(C // H) ** -0.5
    SCALE1 = 1.0 / (WSCALE * WSCALE)

    with ExitStack() as ctx:
        def sb(name, shape, dt):
            return ctx.enter_context(nc.sbuf_tensor(name, shape, dt))

        def sem(name):
            return ctx.enter_context(nc.semaphore(name))

        proj = ctx.enter_context(nc.psum_tensor("proj", [P, 2, 512], F32))
        mps = ctx.enter_context(nc.psum_tensor("mps", [P, 2, 512], F32))
        sps = ctx.enter_context(nc.psum_tensor("sps", [P, 2, 512], F32))
        ops = ctx.enter_context(nc.psum_tensor("ops", [P, 2, 512], F32))

        ident = sb("ident", [P, P], F32)
        ones = sb("ones", [P, P], F32)
        mask = sb("mask", [P, 4], F32)
        wraw0 = sb("wraw0", [P, 10, C], F32)
        wt0 = sb("wt0", [P, 10, C], F16)
        wqd0 = sb("wqd0", [P, KT, 4, P], F16)
        wsum = sb("wsum", [P, 4], F32)
        gam = sb("gam", [P, 4], F32)
        thr = sb("thr", [P, 4], F32)
        nthr = sb("nthr", [P, 4], F32)
        wraw1 = sb("wraw1", [P, 2, 2048], F32)
        wh1 = sb("wh1", [P, 4, 2048], F16)
        wl1 = sb("wl1", [P, 4, 2048], F16)
        bqd = sb("bqd", [P, 4], F32)
        bkp = sb("bkp", [P, KT], F32)
        bvp = sb("bvp", [P, 4], F32)
        bob = sb("bob", [P, C], F32)
        lngp = sb("lngp", [P, KT], F32)
        lnbp = sb("lnbp", [P, KT], F32)
        nwp = sb("nwp", [P, KT], F32)

        ctx32 = sb("ctx32", [P, KT, S], F32)
        ctxh = sb("ctxh", [P, 2, KT, S], F16)
        ctxl = sb("ctxl", [P, 2, KT, S], F16)
        k32 = [sb("k32_0", [P, 2, S], F32), sb("k32_1", [P, 4, S], F32)]
        KA = [sb("KA0", [P, 4, S], F16), sb("KA1", [P, H, S], F16)]
        KB = [sb("KB0", [P, 4, S], F16), sb("KB1", [P, H, S], F16)]
        qA = [sb("qA0", [P, H, T], F16), sb("qA1", [P, H, T], F16)]
        qB = [sb("qB0", [P, H, T], F16), sb("qB1", [P, H, T], F16)]
        V0 = sb("V0", [P, 3, H, 32], F32)
        V1 = sb("V1", [P, 3, H, D1 + 1], F32)
        x32 = sb("x32", [P, C], F32)
        xb = sb("xb", [P, C], F32)
        x1 = sb("x1", [P, 2, C], F32)
        xout = sb("xout", [P, C], F32)
        stats = [sb(f"stats{l}", [P, 6], F32) for l in range(2)]
        mv = [sb(f"mv{l}", [P, 2], F32) for l in range(2)]
        small = [sb(f"small{l}", [P, 8], F32) for l in range(2)]
        xn = [sb(f"xn{l}", [P, C], F32) for l in range(2)]
        xT32 = [sb(f"xT32_{l}", [P, KT, T], F32) for l in range(2)]
        xTh = [sb(f"xTh{l}", [P, KT, T], F16) for l in range(2)]
        xTl = [sb(f"xTl{l}", [P, KT, T], F16) for l in range(2)]
        q32 = sb("q32", [P, 2, 4, T], F32)
        q32_0 = sb("q32_0", [P, 4, T], F32)
        qh0 = sb("qh0", [P, 4, T], F16)
        ql0 = sb("ql0", [P, 4, T], F16)
        gate = sb("gate", [P, 4], F32)
        mx = [sb(f"mx{l}", [P, H], F32) for l in range(2)]
        mT = [sb(f"mT{l}", [P, T], F16) for l in range(2)]
        prob = sb("prob", [P, 4, G], F32)
        wtmp0 = prob[:, :, 0:C]
        rec0 = sb("rec0", [P, 2, 2 * T], F32)
        rcp0 = sb("rcp0", [P, 2, 2 * T], F32)
        on0 = sb("on0", [P, 4, T], F32)
        o32_0 = sb("o32_0", [P, 4, T], F32)
        oh0 = sb("oh0", [P, 4, T], F16)
        ol0 = sb("ol0", [P, 4, T], F16)
        rcp1 = sb("rcp1", [P, H], F32)
        on1 = sb("on1", [P, H * D1], F32)
        o32_1 = sb("o32_1", [P, 8, T], F32)
        oh1 = sb("oh1", [P, 8, T], F16)
        ol1 = sb("ol1", [P, 8, T], F16)

        const_in = sem("const_in")
        w0_in = sem("w0_in")
        w1_in = [sem(f"w1_in{i}") for i in range(2)]
        pad_zero = sem("pad_zero")
        setup_pool = sem("setup_pool")
        setup_ones = sem("setup_ones")
        setup_fill = sem("setup_fill")
        w_sum = sem("w_sum")
        gam_mm = sem("gam_mm")
        gam_ok = sem("gam_ok")
        w_step = sem("w_step")
        w0_ok = sem("w0_ok")
        w1_hi = sem("w1_hi")
        w1_lo = sem("w1_lo")
        proj_full = [sem(f"proj_full{i}") for i in range(2)]
        proj_read = [sem(f"proj_read{i}") for i in range(2)]
        ctx_in = sem("ctx_in")
        ctx_hi = sem("ctx_hi")
        ctx_split = sem("ctx_split")
        k0_hi = sem("k0_hi")
        k_lo = [sem(f"k_lo{l}") for l in range(2)]
        kb_in = [sem(f"kb_in{l}") for l in range(2)]
        x_in = sem("x_in")
        xb_ready = sem("xb_ready")
        st_done = [sem(f"st_done{l}") for l in range(2)]
        ag_done = [sem(f"ag_done{l}") for l in range(2)]
        ms_done = sem("ms_done")
        ve_done = [sem(f"ve_done{l}") for l in range(2)]
        ln_done = [sem(f"ln_done{l}") for l in range(2)]
        rs_done = [sem(f"rs_done{l}") for l in range(2)]
        nw_done = [sem(f"nw_done{l}") for l in range(2)]
        xn_ready = [sem(f"xn_ready{l}") for l in range(2)]
        xTh_ready = [sem(f"xTh_ready{l}") for l in range(2)]
        xTl_ready = [sem(f"xTl_ready{l}") for l in range(2)]
        qA1_ready = sem("qA1_ready")
        qB1_ready = sem("qB1_ready")
        qh0_ready = sem("qh0_ready")
        ql0_ready = sem("ql0_ready")
        qA0_ready = sem("qA0_ready")
        q0_ready = sem("q0_ready")
        max_full = [sem(f"max_full{l}") for l in range(2)]
        max_done = [sem(f"max_done{l}") for l in range(2)]
        mrow_in = [sem(f"mrow_in{l}") for l in range(2)]
        s_full = [sem(f"s_full{l}") for l in range(2)]
        exp_done = [sem(f"exp_done{l}") for l in range(2)]
        prob_used = [sem(f"prob_used{l}") for l in range(2)]
        o_done = [sem(f"o_done{l}") for l in range(2)]
        shuf_done = sem("shuf_done")
        rcp0_done = sem("rcp0_done")
        o32_0_ready = sem("o32_0_ready")
        oh0_ready = sem("oh0_ready")
        ol0_ready = sem("ol0_ready")
        rcp1_done = sem("rcp1_done")
        oh1_ready = sem("oh1_ready")
        ol1_ready = sem("ol1_ready")
        out_stored = sem("out_stored")

        N_CONST_DMA = 2 + 1 + 4 + 3 + 1
        N_W0_DMA = 3 + 4
        EARLY = 6

        block = ctx.enter_context(nc.Block())

        def filled(eng, name, b):
            i, before = turn(name, b, LAST)
            eng.wait_ge(proj_full[i], before + 1)

        def taken(eng, name, b):
            i, before = turn(name, b, LAST)
            eng.wait_ge(proj_read[i], before + 1)

        def place0(s, j):
            return 8 * (s % 2) + 4 * (s // 2) + j

        def heads1(g):
            return range(4 * g, 4 * g + 4)

        @block.sync
        def _(sp):
            sp.dma_start(x32[0:T, :], x[0]).then_inc(x_in, 16)
            sp.dma_start(ctx32[:], ctxT[0].rearrange("(k p) s -> p k s", p=P)).then_inc(ctx_in, 16)
            for i, w in enumerate((WqT0, WkT0, WvT0)):
                sp.dma_start(wraw0[:, 2 * i:2 * i + 2, :], w.rearrange("(k p) n -> p k n", p=P)).then_inc(w0_in, 16)
            sp.wait_ge(pad_zero, 1)
            sp.wait_ge(pad_zero, 1)
            wo_heads = WoT0.rearrange("(s j d) n -> j d s n", j=4, d=16)
            for j in range(4):
                sp.dma_start(wraw0[32 * j:32 * j + 16, 6:10, :], wo_heads[j]).then_inc(w0_in, 16)
            for half in range(2):
                sp.dma_start(bqd[64 * half:64 * half + 64, :], bq).then_inc(const_in, 16)
            sp.dma_start(bkp[:], bk).then_inc(const_in, 16)
            for j in range(4):
                sp.dma_start(bvp[32 * j:32 * j + 16, :], bv[j]).then_inc(const_in, 16)
            sp.dma_start(lngp[:], ln_g).then_inc(const_in, 16)
            sp.dma_start(lnbp[:], ln_b).then_inc(const_in, 16)
            sp.dma_start(nwp[:], norm_w).then_inc(const_in, 16)
            sp.dma_start(bob[0:T, :], bo.broadcast_to([T, C])).then_inc(const_in, 16)

            def load_w1(i, w):
                if i >= 2:
                    sp.wait_ge(w1_lo, i - 1)
                sp.dma_start(wraw1[:, i % 2, :].rearrange("p (k n) -> p k n", n=w.shape[1]),
                             w.rearrange("(k p) n -> p k n", p=P)).then_inc(w1_in[i % 2], 16)

            load_w1(0, wk1)
            load_w1(1, wq1)

            def copy_kb(layer, tiles):
                for odd in range(2):
                    r = slice(64 * odd, 64 * odd + 64)
                    sp.dma_start(KB[layer][r, odd:tiles:2, :], KA[layer][r, odd:tiles:2, :]).then_inc(kb_in[layer], 16)

            def load(n):
                sp.wait_ge(ctx_split, n)
                sp.dma_start(ctx32[:], ctxT[n].rearrange("(k p) s -> p k s", p=P)).then_inc(ctx_in, 16)

            def load_x(n):
                sp.wait_ge(xb_ready, n)
                sp.dma_start(x32[0:T, :], x[n]).then_inc(x_in, 16)

            def rows0(n):
                taken(sp, "mT0", n)
                for odd in range(2):
                    r = 0 if odd else 64
                    sp.dma_start(qB[0][r:r + 1, 8 * odd:8 * odd + 8, :], mT[0][8 * odd:8 * odd + 8, :]
                                 ).then_inc(mrow_in[0], 16)

            def rows1(b):
                taken(sp, "mT1", b)
                for odd in range(2):
                    r = 0 if odd else 64
                    sp.dma_start(qB[1][r:r + 1, odd:H:2, :], mT[1][odd:H:2, :]).then_inc(mrow_in[1], 16)

            def store(b):
                taken(sp, "O1", b)
                sp.dma_start(out[b], xout[0:T, :]).then_inc(out_stored, 16)

            def copy_kb0(n):
                sp.wait_ge(k0_hi, n * 2 + 2)
                copy_kb(0, 4)

            def body(b, n, m):
                if m is not None:
                    load_x(m)
                    load(m)
                if b is None:
                    load_w1(2, wv1)
                    load_w1(3, wo1)
                if b is not None:
                    rows1(b)
                if m is not None:
                    copy_kb0(m)
                if b is not None:
                    store(b)
                if n is not None:
                    if b is None:
                        sp.wait_ge(setup_fill, 2)
                    taken(sp, "K1.7", n)
                    copy_kb(1, H)
                if m is not None:
                    rows0(m)

            sp.wait_ge(setup_fill, 1)
            copy_kb0(0)
            rows0(0)
            body(None, 0, 1)
            with sp.Fori(0, LAST // 2) as pair:
                for i in range(2):
                    body(2 * pair + i, 2 * pair + i + 1, 2 * pair + i + 2)
            body(LAST - 1, LAST, None)
            body(LAST, None, None)
            sp.wait_ge(out_stored, 16 * B + 16)

        @block.tensor
        def _(pe):
            def take(name, b):
                i, before = turn(name, b, LAST)
                pe.wait_ge(proj_read[i], before)
                return proj[:, i, :], proj_full[i]

            def weight_sums():
                pe.wait_ge(setup_ones, 1)
                pe.wait_ge(w_sum, 4)
                pe.matmul(mps[:, 0, 0:4], ones[:], wsum[:], start=True, stop=True).then_inc(gam_mm, 1)

            def key_tile0(t, b, parity):
                bank, full = take(f"K0.{t}", b)
                for n, (k, c) in enumerate((k, c) for k in range(KT) for c in (ctxh, ctxl)):
                    mm = pe.matmul(bank[:, 0:S], wt0[:, 2 + k, P * t:P * t + P], c[:, parity, k, :],
                                   start=n == 0, stop=n == 2 * KT - 1)
                mm.then_inc(full, 1)

            def value_tile0(c, b, parity):
                at, rows = CH[c]
                bank, full = take(f"V0.{c}", b)
                for n, (k, cc) in enumerate((k, cc) for k in range(KT) for cc in (ctxh, ctxl)):
                    mm = pe.matmul(bank[0:rows, 0:C], cc[:, parity, k, at:at + rows], wt0[:, 4 + k, :],
                                   start=n == 0, stop=n == 2 * KT - 1)
                mm.then_inc(full, 1)

            def transpose_x(layer, b):
                bank, full = take(f"xT{layer}", b)
                pe.wait_ge(xn_ready[layer], b + 1)
                for k in range(KT):
                    mm = pe.transpose(bank[:, T * k:T * k + T], xn[layer][0:T, P * k:P * k + P], ident[0:T, 0:T])
                mm.then_inc(full, 1)

            def queries0(b):
                bank, full = take("q0", b)
                pe.wait_ge(xTl_ready[0], b + 1)
                for s in range(4):
                    for n, (k, xx) in enumerate((k, xx) for k in range(KT) for xx in (xTh[0], xTl[0])):
                        mm = pe.matmul(bank[:, T * s:T * s + T], wqd0[:, k, s, :], xx[:, k, :],
                                       start=n == 0, stop=n == 2 * KT - 1)
                mm.then_inc(full, 1)

            def three(k, wi, cols, data_h, data_l):
                h, l = wh1[:, wi, :], wl1[:, wi, :]
                at = 1024 * k
                w = slice(at + cols[0], at + cols[1])
                return [(h[:, w], data_h), (h[:, w], data_l), (l[:, w], data_h)]

            def key_tile1(j, b, parity):
                bank, full = take(f"K1.{j}", b)
                pairs = [p for k in range(KT)
                         for p in three(k, 0, (P * j, P * j + P), ctxh[:, parity, k, :], ctxl[:, parity, k, :])]
                for n, (w, c) in enumerate(pairs):
                    mm = pe.matmul(bank[:, 0:S], w, c, start=n == 0, stop=n == len(pairs) - 1)
                mm.then_inc(full, 1)

            def value_tile1(u, b, parity, early=()):
                bank, full = take(f"V1.{u}", b)
                at, rows = CH[u // 2]
                cols = (512 * (u % 2), 512 * (u % 2) + 512)
                pairs = [p for k in range(KT)
                         for p in three(k, 2, cols, ctxh[:, parity, k, at:at + rows], ctxl[:, parity, k, at:at + rows])]
                for n, (w, c) in enumerate(pairs):
                    if n == len(pairs) // 2:
                        rows1(early, b)
                    mm = pe.matmul(bank[0:rows, :], c, w, start=n == 0, stop=n == len(pairs) - 1)
                mm.then_inc(full, 1)

            def queries1(half, b):
                pe.wait_ge(xTl_ready[1], b + 1)
                bank, full = take(f"q1.{half}", b)
                for i in range(4):
                    j = 4 * half + i
                    pairs = [p for k in range(KT)
                             for p in three(k, 1, (P * j, P * j + P), xTh[1][:, k, :], xTl[1][:, k, :])]
                    for n, (w, xx) in enumerate(pairs):
                        mm = pe.matmul(bank[:, T * i:T * i + T], w, xx, start=n == 0, stop=n == len(pairs) - 1)
                mm.then_inc(full, 1)

            def row_scores(layer, h, b):
                if h >= 2:
                    pe.wait_ge(max_done[layer], b * H + h - 1)
                if layer == 1:
                    pe.wait_ge(k_lo[1], b * H + h + 1)
                tile = KA[layer][:, h if layer else h // 4, :]
                pe.matmul(mps[0:T, h % 2, 0:S], qA[layer][:, h, :], tile, start=True, stop=True
                          ).then_inc(max_full[layer], 1)

            def transpose_max(layer, b):
                bank, full = take(f"mT{layer}", b)
                pe.wait_ge(max_done[layer], b * H + H)
                pe.transpose(bank[0:H, 0:T], mx[layer][0:T, :], ident[0:T, 0:T]).then_inc(full, 1)

            def scores(layer, u, b):
                g, c = u // 3, u % 3
                at, rows = CH[c]
                if u >= 2:
                    pe.wait_ge(exp_done[layer], b * 12 + u - 1)
                if layer == 0:
                    pe.matmul(sps[0:rows, u % 2, 0:G], KA[0][:, g, at:at + rows],
                              qA[0][:, 4 * g:4 * g + 4, :], start=True, stop=False)
                    mm = pe.matmul(sps[0:rows, u % 2, 0:G], KB[0][:, g, at:at + rows],
                                   qB[0][:, place0(g, 0):place0(g, 3) + 1, :], start=False, stop=True)
                else:
                    for i, h in enumerate(heads1(g)):
                        o = sps[0:rows, u % 2, T * i:T * i + T]
                        pe.matmul(o, KA[1][:, h, at:at + rows], qA[1][:, h, :], start=True, stop=False)
                        mm = pe.matmul(o, KB[1][:, h, at:at + rows], qB[1][:, h, :], start=False, stop=True)
                mm.then_inc(s_full[layer], 1)

            def weigh(layer, u, b, with_layer0=False):
                g, c = u // 3, u % 3
                rows = CH[c][1]
                pe.wait_ge(exp_done[layer], b * 12 + u + 1)
                p = prob[0:rows, u % 4, :]
                if layer == 1 and c == 0 and g >= 2:
                    pe.wait_ge(o_done[1], b * 4 + g - 1)
                elif layer == 1 and c == 0 and with_layer0:
                    pe.wait_ge(o_done[0], b * 2 + 2 + g + 1)
                if layer == 0:
                    for j in range(4):
                        mm = pe.matmul(ops[32 * j:32 * j + 32, g // 2, T * (g % 2):T * (g % 2) + T],
                                       V0[0:rows, c, 4 * g + j, :], p[:, T * j:T * j + T],
                                       start=c == 0, stop=c == 2, tile_position=(0, 32 * j))
                else:
                    for i, h in enumerate(heads1(g)):
                        mm = pe.matmul(ops[0:T, g % 2, (D1 + 1) * i:(D1 + 1) * (i + 1)], p[:, T * i:T * i + T],
                                       V1[0:rows, c, h, :], start=c == 0 and i == 0, stop=c == 2,
                                       skip_group_check=True)
                mm.then_inc(prob_used[layer], 1)

            def transpose_out(half, b):
                bank, full = take(f"oT{half}", b)
                pe.wait_ge(o_done[1], b * 4 + 2 * half + 2)
                for i in range(4):
                    at = P * (4 * half + i)
                    mm = pe.transpose(bank[:, T * i:T * i + T], on1[0:T, at:at + P], ident[0:T, 0:T])
                mm.then_inc(full, 1)

            def project_out(layer, b):
                bank, full = take(f"O{layer}", b)
                if layer == 0:
                    pe.wait_ge(ol0_ready, b * 2 + 2)
                    for n, (s, oo) in enumerate((s, oo) for s in range(4) for oo in (oh0, ol0)):
                        mm = pe.matmul(bank[0:T, 0:C], oo[:, s, :], wt0[:, 6 + s, :], start=n == 0, stop=n == 7)
                else:
                    for k in range(8):
                        if k in (0, 4):
                            pe.wait_ge(ol1_ready, b * 2 + k // 4 + 1)
                        w = slice(C * k, C * k + C)
                        for n, (oo, ww) in enumerate(((oh1, wh1), (oh1, wl1), (ol1, wh1))):
                            mm = pe.matmul(bank[0:T, 0:C], oo[:, k, :], ww[:, 3, w],
                                           start=k == 0 and n == 0, stop=k == 7 and n == 2)
                mm.then_inc(full, 1)

            def rows1(heads, b):
                if b is not None:
                    for h in heads:
                        row_scores(1, h, b)

            def rows0(heads, m):
                if m is not None:
                    for h in heads:
                        row_scores(0, h, m)

            def body(b, n, m, parity):
                rows1(range(EARLY, EARLY + 1), b)
                if n is not None:
                    pe.wait_ge(mrow_in[0], n * 32 + 32)
                    pe.wait_ge(q0_ready, n + 1)
                    pe.wait_ge(kb_in[0], n * 32 + 32)
                    scores(0, 0, n)
                rows1(range(EARLY + 1, EARLY + 2), b)
                if n is not None:
                    scores(0, 1, n)
                for u in range(12):
                    h = EARLY + 2 + 2 * u
                    rows1(range(h, min(h + 1, H)), b)
                    if n is not None:
                        weigh(0, u, n)
                    rows1(range(h + 1, min(h + 2, H)), b)
                    if n is not None and u < 10:
                        scores(0, u + 2, n)
                    if b is not None and u == 4:
                        transpose_max(1, b)
                    if m is not None and u == 8:
                        transpose_x(0, m)
                    if b is not None and u == 9:
                        value_tile1(4, b, 1 - parity)
                if b is not None:
                    value_tile1(5, b, 1 - parity)

                if b is not None:
                    pe.wait_ge(mrow_in[1], b * 32 + 32)
                    pe.wait_ge(qB1_ready, b * 4 + 4)
                    pe.wait_ge(kb_in[1], b * 32 + 32)
                    scores(1, 0, b)
                    scores(1, 1, b)
                if m is not None:
                    queries0(m)
                for u in range(12):
                    if b is not None:
                        weigh(1, u, b, n is not None)
                    if m is not None:
                        if u == 2:
                            pe.wait_ge(ctx_split, m + 1)
                            value_tile0(0, m, 1 - parity)
                        if u in (3, 6):
                            key_tile0((u - 3) // 3, m, 1 - parity)
                        if u == 7:
                            value_tile0(1, m, 1 - parity)
                        if u == 10:
                            value_tile0(2, m, 1 - parity)
                    if n is not None and u == 4:
                        project_out(0, n)
                    if b is not None and u < 10:
                        scores(1, u + 2, b)
                    if n is not None and u == 8:
                        transpose_x(1, n)
                    if b is not None and u == 9:
                        transpose_out(0, b)

                if n is None:
                    transpose_out(1, b)
                    project_out(1, b)
                else:
                    if b is None:
                        pe.wait_ge(w1_lo, 2)
                    queries1(0, n)
                    if b is not None:
                        transpose_out(1, b)
                    key_tile1(0, n, parity)
                    queries1(1, n)
                    key_tile1(1, n, parity)
                    if m is not None:
                        pe.wait_ge(k_lo[0], m * 4 + 4)
                        pe.wait_ge(qA0_ready, m + 1)
                    rows0(range(0, 2), m)
                    key_tile1(2, n, parity)
                    rows0(range(2, 4), m)
                    if b is not None:
                        project_out(1, b)
                    for j in range(3, 8):
                        rows0(range(2 * j - 2, 2 * j), m)
                        key_tile1(j, n, parity)
                    if b is None:
                        pe.wait_ge(w1_lo, 3)
                    rows0(range(14, H), m)
                    value_tile1(0, n, parity)
                    if m is not None:
                        transpose_max(0, m)
                    pe.wait_ge(qA1_ready, n * 2 + 2)
                    for u in range(1, 4):
                        rows1(range(4 * u - 4, min(4 * u - 2, EARLY)), n)
                        value_tile1(u, n, parity, range(4 * u - 2, min(4 * u, EARLY)))

            pe.wait_ge(setup_pool, 7)
            transpose_x(0, 0)
            weight_sums()
            pe.wait_ge(w0_ok, 1)
            queries0(0)
            pe.wait_ge(ctx_split, 1)
            value_tile0(0, 0, 0)
            for t in range(2):
                key_tile0(t, 0, 0)
            for c in range(1, 3):
                value_tile0(c, 0, 0)
            pe.wait_ge(k_lo[0], 4)
            pe.wait_ge(qA0_ready, 1)
            rows0(range(H), 0)
            transpose_max(0, 0)
            body(None, 0, 1, 0)
            pe.wait_ge(setup_fill, 2)
            with pe.Fori(0, LAST // 2) as pair:
                for i in range(2):
                    body(2 * pair + i, 2 * pair + i + 1, 2 * pair + i + 2, 1 - i)
            body(LAST - 1, LAST, None, 1)
            body(LAST, None, None, 0)

        @block.scalar
        def _(act):
            def full(name, b):
                i, before = turn(name, b, LAST)
                act.wait_ge(proj_full[i], before + 1)
                return proj[:, i, :], proj_read[i]

            def key_tile(layer, t, scale, bias, b):
                bank, free = full(f"K{layer}.{t}", b)
                slots, tiles = (4, 8) if layer else (2, 2)
                if not isinstance(b, int) or b * tiles + t >= slots:
                    act.wait_ge(k_lo[layer], 2 * (b * tiles + t - slots + 1))
                slot = k32[layer][:, t % slots, :]
                if layer == 1:
                    for half in range(2):
                        r = slice(64 * half, 64 * half + 64)
                        nc.scalar.activation(KA[1][r, 2 * t + half, :], bank[r, 0:S], ACT.Copy)
                nc.scalar.activation(slot, bank[:, 0:S], ACT.Identity, scale=scale, bias=bias
                                     ).then_inc(free, 1)

            def values0(c, b):
                bank, free = full(f"V0.{c}", b)
                rows = CH[c][1]
                nc.scalar.activation(V0[0:rows, c, :, 0:16], bank[0:rows, 0:C].rearrange("p (h d) -> p h d", d=16),
                                     ACT.Copy).then_inc(free, 1)

            def values1(u, b):
                bank, free = full(f"V1.{u}", b)
                rows = CH[u // 2][1]
                at = 8 * (u % 2)
                nc.scalar.activation(V1[0:rows, u // 2, at:at + 8, 0:D1],
                                     bank[0:rows, :].rearrange("p (h d) -> p h d", d=D1), ACT.Copy).then_inc(free, 1)

            def row_max(layer, b):
                bank, free = full(f"mT{layer}", b)
                nc.scalar.activation(mT[layer][0:H, :], bank[0:H, 0:T], ACT.Copy, scale=-1.0 / MROW
                                     ).then_inc(free, 1)

            def rsqrt(layer, nb):
                act.wait_ge(ve_done[layer], nb + 1)
                s = small[layer]
                nc.scalar.activation(s[0:T, 1:2], s[0:T, 0:1], ACT.Ln).then_inc(ln_done[layer], 1)
                act.wait_ge(ln_done[layer], nb + 1)
                nc.scalar.activation(s[0:T, 2:3], s[0:T, 1:2], ACT.Exp, scale=-0.5).then_inc(rs_done[layer], 1)

            def transposed_x(layer, b):
                bank, free = full(f"xT{layer}", b)
                if layer == 0:
                    for k in range(KT):
                        i = nc.scalar.activation(xT32[0][:, k, :], bank[:, T * k:T * k + T], ACT.Identity,
                                                 scale=lngp[:, k:k + 1], bias=lnbp[:, k:k + 1])
                else:
                    for k in range(KT):
                        i = nc.scalar.activation(xT32[1][:, k, :], bank[:, T * k:T * k + T], ACT.Identity,
                                                 scale=nwp[:, k:k + 1])
                i.then_inc(free, 1)

            def queries1(half, b):
                bank, free = full(f"q1.{half}", b)
                nc.scalar.activation(q32[:, half, :, :], bank[:, 0:G].rearrange("p (j t) -> p j t", t=T),
                                     ACT.Copy).then_inc(free, 1)

            def exp(layer, u, b):
                rows = CH[u % 3][1]
                act.wait_ge(s_full[layer], b * 12 + u + 1)
                if u >= 4:
                    act.wait_ge(prob_used[layer], b * 12 + u - 3)
                nc.scalar.activation(prob[0:rows, u % 4, :], sps[0:rows, u % 2, 0:G], ACT.Exp,
                                     scale=SCALE1 if layer else SCALE0).then_inc(exp_done[layer], 1)

            def output1(half, b):
                bank, free = full(f"oT{half}", b)
                nc.scalar.activation(o32_1[:, 4 * half:4 * half + 4, :],
                                     bank[:, 0:G].rearrange("p (k t) -> p k t", t=T), ACT.Copy).then_inc(free, 1)

            def output0(i, n):
                act.wait_ge(o_done[0], n * 2 + i + 1)
                for s in range(2 * i, 2 * i + 2):
                    ins = nc.scalar.activation(o32_0[:, s, :], on0[:, s, :], ACT.Identity,
                                               scale=gam[:, 2:3], bias=bvp[:, s:s + 1])
                ins.then_inc(o32_0_ready, 1)

            def split_ctx_hi(n, parity):
                act.wait_ge(ctx_in, n * 16 + 16)
                nc.scalar.activation(ctxh[:, parity], ctx32[:], ACT.Copy).then_inc(ctx_hi, 1)

            def w1_part(i):
                act.wait_ge(w1_in[i % 2], 16 * (i // 2 + 1))
                nc.scalar.activation(wh1[:, i, :], wraw1[:, i % 2, :], ACT.Copy, scale=WSCALE).then_inc(w1_hi, 1)

            def key_tile0(t, m):
                key_tile(0, t, gam[:, 1:2], bkp[:, t:t + 1], m)

            def body(b, n, m, parity):
                for u in range(12):
                    if n is not None:
                        exp(0, u, n)
                    if u == 5 and b is not None:
                        row_max(1, b)
                    if u == 6 and m is not None:
                        rsqrt(0, m)
                    if u == 9 and m is not None:
                        transposed_x(0, m)
                if b is not None:
                    values1(4, b)
                for u in range(12):
                    if b is not None:
                        exp(1, u, b)
                    if b is not None and u == 0:
                        values1(5, b)
                    if m is not None and u == 0:
                        split_ctx_hi(m, 1 - parity)
                    if n is not None and u in (1, 2):
                        output0(u - 1, n)
                    if n is not None and u == 10:
                        transposed_x(1, n)
                    if b is not None and u == 11:
                        output1(0, b)
                    if m is not None:
                        if u == 3:
                            values0(0, m)
                        if u in (4, 7):
                            key_tile0((u - 4) // 3, m)
                        if u == 8:
                            values0(1, m)
                        if u == 11:
                            values0(2, m)
                    if n is not None and u == 6:
                        rsqrt(1, n)
                    if b is None and u in (2, 5):
                        w1_part(2 + u // 5)
                if n is None:
                    output1(1, b)
                else:
                    for half in range(2):
                        queries1(half, n)
                        if b is not None and half == 0:
                            output1(1, b)
                        key_tile(1, half, 1.0, 0.0, n)
                    for j in range(2, 8):
                        key_tile(1, j, 1.0, 0.0, n)
                    values1(0, n)
                    if m is not None:
                        row_max(0, m)
                    values1(1, n)
                    values1(2, n)
                    values1(3, n)

            nc.scalar.preload_act_table_set("natural_log_exp_and_others")
            rsqrt(0, 0)
            split_ctx_hi(0, 0)
            act.wait_ge(const_in, 16 * N_CONST_DMA)
            transposed_x(0, 0)
            act.wait_ge(gam_ok, 1)
            values0(0, 0)
            for t in range(2):
                key_tile0(t, 0)
            for c in range(1, 3):
                values0(c, 0)
            w1_part(0)
            w1_part(1)
            row_max(0, 0)
            body(None, 0, 1, 0)
            with act.Fori(0, LAST // 2) as pair:
                for i in range(2):
                    body(2 * pair + i, 2 * pair + i + 1, 2 * pair + i + 2, 1 - i)
            body(LAST - 1, LAST, None, 1)
            body(LAST, None, None, 0)

        @block.vector
        def _(dve):
            steps = [0]

            def step(ins):
                steps[0] += 1
                ins.then_inc(w_step, 1)
                dve.wait_ge(w_step, steps[0])

            def key_tile0(t, b):
                taken(dve, f"K0.{t}", b)
                nc.vector.tensor_copy(KA[0][0:64, 2 * t, :], k32[0][0:64, t, :])
                nc.vector.tensor_copy(KA[0][64:P, 2 * t + 1, :], k32[0][64:P, t, :]).then_inc(k0_hi, 1)

            def statistics(layer, nb, parity=0):
                src = x1[0:T, parity, :] if layer else x32[0:T, :]
                nc.vector.bn_stats(out=stats[layer][0:T, :], in_=src).then_inc(st_done[layer], 1)
                dve.wait_ge(st_done[layer], nb + 1)
                nc.vector.memset(gate[0:1, layer:layer + 1], 0.0)
                m = mv[layer]
                nc.vector.bn_aggr(out=m[0:T, :], in_=stats[layer][0:T, :]).then_inc(ag_done[layer], 1)
                dve.wait_ge(ag_done[layer], nb + 1)
                s = small[layer]
                var = m[0:T, 1:2]
                if layer:
                    nc.vector.scalar_tensor_tensor(out=s[0:T, 3:4], in0=m[0:T, 0:1], scalar=m[0:T, 0:1],
                                                   in1=m[0:T, 1:2], op0=ALU.mult, op1=ALU.add).then_inc(ms_done, 1)
                    dve.wait_ge(ms_done, nb + 1)
                    var = s[0:T, 3:4]
                nc.vector.tensor_scalar(s[0:T, 0:1], var, RMS_EPS if layer else LN_EPS, None, ALU.add
                                        ).then_inc(ve_done[layer], 1)

            def normalise_x(layer, nb, parity=0):
                s, n = small[layer], nw_done[layer]
                y = s[0:T, 2:3]
                dve.wait_ge(rs_done[layer], nb + 1)
                nc.vector.tensor_tensor(s[0:T, 4:5], y, y, ALU.mult).then_inc(n, 1)
                dve.wait_ge(n, nb * 3 + 1)
                nc.vector.tensor_scalar(s[0:T, 5:6], s[0:T, 4:5], s[0:T, 0:1], -0.5, ALU.mult, ALU.mult).then_inc(n, 1)
                dve.wait_ge(n, nb * 3 + 2)
                nc.vector.tensor_scalar(s[0:T, 6:7], s[0:T, 5:6], 1.5, y, ALU.add, ALU.mult).then_inc(n, 1)
                dve.wait_ge(n, nb * 3 + 3)
                if layer:
                    i = nc.vector.tensor_scalar(xn[1][0:T, :], x1[0:T, parity, :], s[0:T, 6:7], None, ALU.mult)
                else:
                    i = nc.vector.tensor_scalar(xn[0][0:T, :], x32[0:T, :], mv[0][0:T, 0:1], s[0:T, 6:7],
                                                ALU.subtract, ALU.mult)
                i.then_inc(xn_ready[layer], 1)

            def x_hi(layer, b):
                taken(dve, f"xT{layer}", b)
                nc.vector.tensor_copy(xTh[layer][:], xT32[layer][:]).then_inc(xTh_ready[layer], 1)

            def queries0_hi(nb):
                filled(dve, "q0", nb)
                bank, _ = turn("q0", nb, LAST)
                for s in range(4):
                    i = nc.vector.tensor_scalar(q32_0[:, s, :], proj[:, bank, T * s:T * s + T], gam[:, 0:1],
                                                bqd[:, s:s + 1], ALU.mult, ALU.add)
                i.then_inc(proj_read[bank], 1)
                taken(dve, "q0", nb)
                nc.vector.tensor_copy(qh0[:], q32_0[:]).then_inc(qh0_ready, 1)

            def mask_queries0_hi(nb):
                dve.wait_ge(qh0_ready, nb + 1)
                for j in range(4):
                    i = nc.vector.tensor_scalar(qA[0][:, j:H:4, :], qh0[:], mask[:, j:j + 1], None, ALU.mult)
                i.then_inc(qA0_ready, 1)

            def mask_queries0_lo(nb):
                dve.wait_ge(ql0_ready, nb + 1)
                for j in range(4):
                    for odd in range(2):
                        r = slice(64 * odd, 64 * odd + 64)
                        i = nc.vector.tensor_scalar(qB[0][r, 8 * odd + j:8 * odd + 8:4, :], ql0[r, odd:4:2, :],
                                                    mask[r, j:j + 1], None, ALU.mult)
                i.then_inc(q0_ready, 1)

            def queries1_hi(half, b):
                taken(dve, f"q1.{half}", b)
                for odd in range(2):
                    r = slice(64 * odd, 64 * odd + 64)
                    for to in range(2):
                        i = nc.vector.tensor_copy(qA[1][64 * to:64 * to + 64, 8 * half + odd:8 * half + 8:2, :],
                                                  q32[r, half, :, :])
                i.then_inc(qA1_ready, 1)

            def row_max(layer, h, b):
                dve.wait_ge(max_full[layer], b * H + h + 1)
                at = h if layer else place0(h // 4, h % 4)
                nc.vector.tensor_reduce(mx[layer][0:T, at:at + 1], mps[0:T, h % 2, 0:S], AX.X, ALU.max
                                        ).then_inc(max_done[layer], 1)

            def normalise0(i, b):
                dve.wait_ge(prob_used[0], b * 12 + 6 * i + 6)
                nc.vector.memset(gate[0:1, 2 + i:3 + i], 0.0)
                src = ops[:, i, 0:2 * T]
                nc.vector.stream_shuffle(rec0[:, i, :], src, list(range(16, 32)) * 2).then_inc(shuf_done, 1)
                dve.wait_ge(shuf_done, b * 2 + i + 1)
                nc.vector.reciprocal(rcp0[:, i, :], rec0[:, i, :]).then_inc(rcp0_done, 1)
                dve.wait_ge(rcp0_done, b * 2 + i + 1)
                nc.vector.tensor_tensor(on0[:, 2 * i:2 * i + 2, :], src.rearrange("p (s t) -> p s t", t=T),
                                        rcp0[:, i, :].rearrange("p (s t) -> p s t", t=T), ALU.mult
                                        ).then_inc(o_done[0], 1)

            def normalise1(g, b):
                dve.wait_ge(prob_used[1], b * 12 + 3 * g + 3)
                bank = ops[0:T, g % 2, 0:4 * (D1 + 1)].rearrange("t (h d) -> t h d", d=D1 + 1)
                nc.vector.reciprocal(rcp1[0:T, 4 * g:4 * g + 4], bank[:, :, D1]).then_inc(rcp1_done, 1)
                dve.wait_ge(rcp1_done, b * 4 + g + 1)
                for i, h in enumerate(heads1(g)):
                    ins = nc.vector.tensor_scalar(on1[0:T, D1 * h:D1 * h + D1], bank[:, i, 0:D1],
                                                  rcp1[0:T, h:h + 1], None, ALU.mult)
                ins.then_inc(o_done[1], 1)

            def output1_hi(half, b):
                taken(dve, f"oT{half}", b)
                at = slice(4 * half, 4 * half + 4)
                nc.vector.tensor_copy(oh1[:, at, :], o32_1[:, at, :]).then_inc(oh1_ready, 1)

            step(nc.vector.memset(wraw0[:, 6:10, :], 0.0))
            nc.vector.memset(bvp[:], 0.0).then_inc(pad_zero, 1)
            nc.vector.memset(gate[:], 0.0).then_inc(out_stored, 16)
            nc.vector.memset(ones[:], 1.0).then_inc(setup_ones, 1)
            dve.wait_ge(x_in, 16)
            statistics(0, 0)
            normalise_x(0, 0)
            dve.wait_ge(w0_in, 16 * N_W0_DMA)
            for i, (a, z) in enumerate(((0, 2), (2, 4), (4, 6), (6, 10))):
                nc.vector.tensor_reduce(wsum[:, i:i + 1], wraw0[:, a:z, :], AX.XY, ALU.add,
                                        apply_absolute_value=True).then_inc(w_sum, 1)
            dve.wait_ge(gam_mm, 1)
            step(nc.vector.tensor_scalar(gam[:], mps[:, 0, 0:4], 1.0 / (C * C), None, ALU.mult))
            step(nc.vector.tensor_scalar(thr[:], gam[:], Q_EPS, 0.5, ALU.add, ALU.mult))
            nc.vector.tensor_scalar(nthr[:], thr[:], -1.0, None, ALU.mult).then_inc(gam_ok, 1)
            dve.wait_ge(gam_ok, 1)
            x_hi(0, 0)
            for i, (a, z) in enumerate(((0, 2), (2, 4), (4, 6), (6, 10))):
                step(nc.vector.tensor_scalar(wtmp0[:, 0:z - a, :], wraw0[:, a:z, :], nthr[:, i:i + 1], None, ALU.is_lt))
                step(nc.vector.scalar_tensor_tensor(out=wt0[:, a:z, :], in0=wraw0[:, a:z, :], scalar=thr[:, i:i + 1],
                                                    in1=wtmp0[:, 0:z - a, :], op0=ALU.is_gt, op1=ALU.subtract))
            for k in range(KT):
                for half in range(2):
                    i = nc.vector.tensor_copy(wqd0[:, k, :, 64 * half:64 * half + 64],
                                              wt0[:, k, :].rearrange("p (s d) -> p s d", d=64))
            i.then_inc(w0_ok, 1)

            def first_residual(n, parity):
                filled(dve, "O0", n)
                dve.wait_ge(xb_ready, n + 1)
                i, _ = turn("O0", n, LAST)
                nc.vector.scalar_tensor_tensor(out=x1[0:T, parity, :], in0=proj[0:T, i, 0:C], scalar=gam[0:T, 3:4],
                                               in1=xb[0:T, :], op0=ALU.mult, op1=ALU.add).then_inc(proj_read[i], 1)
                taken(dve, "O0", n)

            def second_residual(b, parity):
                filled(dve, "O1", b)
                dve.wait_ge(out_stored, b * 16 + 16)
                i, _ = turn("O1", b, LAST)
                nc.vector.scalar_tensor_tensor(out=xout[0:T, :], in0=proj[0:T, i, 0:C], scalar=SCALE1,
                                               in1=x1[0:T, parity, :], op0=ALU.mult, op1=ALU.add
                                               ).then_inc(proj_read[i], 1)

            def maxima(layer, heads, b):
                if b is not None:
                    for h in heads:
                        row_max(layer, h, b)

            def output0_hi(i, n):
                dve.wait_ge(o32_0_ready, n * 2 + i + 1)
                nc.vector.tensor_copy(oh0[:, 2 * i:2 * i + 2, :], o32_0[:, 2 * i:2 * i + 2, :]).then_inc(oh0_ready, 1)

            def w1_part(i):
                dve.wait_ge(w1_hi, i + 1)
                nc.vector.scalar_tensor_tensor(out=wl1[:, i, :], in0=wraw1[:, i % 2, :], scalar=WSCALE,
                                               in1=wh1[:, i, :], op0=ALU.mult, op1=ALU.subtract).then_inc(w1_lo, 1)

            def body(b, n, m, parity):
                maxima(1, range(EARLY, H), b)
                if m is not None:
                    dve.wait_ge(x_in, m * 16 + 16)
                    statistics(0, m)
                    normalise_x(0, m)
                    x_hi(0, m)
                if n is not None:
                    normalise0(0, n)
                if n is not None:
                    normalise0(1, n)
                if m is not None:
                    queries0_hi(m)
                if n is not None:
                    output0_hi(0, n)
                if m is not None:
                    mask_queries0_hi(m)
                if n is not None:
                    output0_hi(1, n)
                if m is not None:
                    mask_queries0_lo(m)
                if b is not None:
                    normalise1(0, b)
                if m is not None:
                    key_tile0(0, m)
                if n is not None:
                    first_residual(n, parity)
                    statistics(1, n, parity)
                if b is not None:
                    normalise1(1, b)
                if n is not None:
                    normalise_x(1, n, parity)
                if m is not None:
                    key_tile0(1, m)
                if b is None:
                    w1_part(2)
                if n is not None:
                    x_hi(1, n)
                if b is not None:
                    normalise1(2, b)
                    output1_hi(0, b)
                if b is not None:
                    normalise1(3, b)
                else:
                    w1_part(3)
                if b is not None:
                    output1_hi(1, b)
                if n is None:
                    second_residual(b, 1 - parity)
                else:
                    maxima(0, range(2), m)
                    queries1_hi(0, n)
                    maxima(0, range(2, 4), m)
                    queries1_hi(1, n)
                    if b is not None:
                        second_residual(b, 1 - parity)
                    maxima(0, range(4, H), m)
                    maxima(1, range(EARLY), n)

            dve.wait_ge(const_in, 16 * N_CONST_DMA)
            queries0_hi(0)
            mask_queries0_hi(0)
            key_tile0(0, 0)
            key_tile0(1, 0)
            dve.wait_ge(setup_fill, 1)
            mask_queries0_lo(0)
            maxima(0, range(H), 0)
            w1_part(0)
            w1_part(1)

            body(None, 0, 1, 0)
            with dve.Fori(0, LAST // 2) as pair:
                for i in range(2):
                    body(2 * pair + i, 2 * pair + i + 1, 2 * pair + i + 2, 1 - i)
            body(LAST - 1, LAST, None, 1)
            body(LAST, None, None, 0)

        @block.gpsimd
        def _(pool):
            def setup(ins, n):
                ins.then_inc(setup_pool, 1)
                pool.wait_ge(setup_pool, n)

            setup(nc.gpsimd.memset(ident[:], 0.0), 1)
            setup(nc.gpsimd.memset(mask[:], 1.0), 2)
            setup(nc.gpsimd.affine_select(out=ident[:], in_=ident[:], compare_op=ALU.not_equal, fill=1.0, base=0,
                                          pattern=[[-1, P]], channel_multiplier=1), 3)
            for half in range(2):
                m = mask[64 * half:64 * half + 64, :]
                setup(nc.gpsimd.affine_select(out=m, in_=m, compare_op=ALU.is_ge, fill=0.0, base=0,
                                              pattern=[[-16, 4]], channel_multiplier=1), 4 + 2 * half)
                setup(nc.gpsimd.affine_select(out=m, in_=m, compare_op=ALU.is_ge, fill=0.0, base=15,
                                              pattern=[[16, 4]], channel_multiplier=-1), 5 + 2 * half)

            filled_tiles = [7]

            def fill(tile, value):
                filled_tiles[0] += 1
                setup(nc.gpsimd.memset(tile, value), filled_tiles[0])

            def fill_rows(layer, ones_of_v):
                fill(KB[layer][64:65, 0::2, :], MROW)
                fill(KB[layer][0:1, 1::2, :], MROW)
                nc.gpsimd.memset(ones_of_v, 1.0).then_inc(setup_fill, 1)
                pool.wait_ge(setup_fill, layer + 1)

            def lo_part(out, a, hi, done, count):
                nc.gpsimd.tensor_tensor(out, a, hi, ALU.subtract).then_inc(done, 1)
                pool.wait_ge(done, count)

            def split_ctx_lo(nb, parity):
                pool.wait_ge(ctx_hi, nb + 1)
                lo_part(ctxl[:, parity], ctx32[:], ctxh[:, parity], ctx_split, nb + 1)

            def key_tile(layer, t, b):
                n = (b * 8 if layer else b * 2) + t
                if layer:
                    taken(pool, f"K1.{t}", b)
                else:
                    pool.wait_ge(k0_hi, n + 1)
                slot = k32[layer][:, t % 4, :]
                k = KA[layer]
                lo_part(k[64:P, 2 * t, :], slot[0:64, :], k[0:64, 2 * t, :], k_lo[layer], n * 2 + 1)
                lo_part(k[0:64, 2 * t + 1, :], slot[64:P, :], k[64:P, 2 * t + 1, :], k_lo[layer], n * 2 + 2)

            def x_lo(layer, nb):
                pool.wait_ge(xTh_ready[layer], nb + 1)
                lo_part(xTl[layer][:], xT32[layer][:], xTh[layer][:], xTl_ready[layer], nb + 1)

            def queries0_lo(nb):
                pool.wait_ge(qh0_ready, nb + 1)
                lo_part(ql0[:], q32_0[:], qh0[:], ql0_ready, nb + 1)

            def output0_lo(i, n):
                two = slice(2 * i, 2 * i + 2)
                pool.wait_ge(oh0_ready, n * 2 + i + 1)
                lo_part(ol0[:, two, :], o32_0[:, two, :], oh0[:, two, :], ol0_ready, n * 2 + i + 1)

            def queries1_lo(half, nb):
                pool.wait_ge(qA1_ready, nb * 2 + half + 1)
                for odd in range(2):
                    r = slice(64 * odd, 64 * odd + 64)
                    heads = slice(8 * half + odd, 8 * half + 8, 2)
                    lo_part(qB[1][r, heads, :], q32[r, half, :, :], qA[1][r, heads, :],
                            qB1_ready, nb * 4 + 2 * half + odd + 1)

            def output1_lo(half, b):
                pool.wait_ge(oh1_ready, b * 2 + half + 1)
                at = slice(4 * half, 4 * half + 4)
                lo_part(ol1[:, at, :], o32_1[:, at, :], oh1[:, at, :], ol1_ready, b * 2 + half + 1)

            def body(b, n, m, parity):
                if n is not None:
                    nc.gpsimd.tensor_tensor(xb[0:T, :], x32[0:T, :], bob[0:T, :], ALU.add).then_inc(xb_ready, 1)
                    pool.wait_ge(xb_ready, n + 1)
                if b is not None:
                    queries1_lo(0, b)
                    queries1_lo(1, b)
                if m is not None:
                    x_lo(0, m)
                    split_ctx_lo(m, 1 - parity)
                    queries0_lo(m)
                if n is not None:
                    output0_lo(0, n)
                    output0_lo(1, n)
                if m is not None:
                    key_tile(0, 0, m)
                    key_tile(0, 1, m)
                if n is not None:
                    x_lo(1, n)
                if b is not None:
                    output1_lo(0, b)
                if b is not None:
                    output1_lo(1, b)
                if n is not None:
                    for j in range(8):
                        key_tile(1, j, n)

            split_ctx_lo(0, 0)
            fill(KB[0][:], 0.0)
            fill(qB[0][:], 0.0)
            fill_rows(0, V0[:, :, :, 16:32])
            x_lo(0, 0)
            queries0_lo(0)
            for t in range(2):
                key_tile(0, t, 0)
            fill(KB[1][:], 0.0)
            fill(qB[1][:], 0.0)
            fill_rows(1, V1[:, :, :, D1:D1 + 1])
            pool.wait_ge(const_in, 16 * N_CONST_DMA)
            pool.wait_ge(x_in, 16)
            body(None, 0, 1, 0)
            with pool.Fori(0, LAST // 2) as pair:
                for i in range(2):
                    body(2 * pair + i, 2 * pair + i + 1, 2 * pair + i + 2, 1 - i)
            body(LAST - 1, LAST, None, 1)
            body(LAST, None, None, 0)


def kernel(x, ctx_1024, L0_xattn_Wq, L0_xattn_bq, L0_xattn_Wk, L0_xattn_bk, L0_xattn_Wv, L0_xattn_bv, L0_xattn_Wo,
           L0_xattn_bo, L0_xattn_ln_gamma, L0_xattn_ln_beta, L1_xattn_wq, L1_xattn_wk, L1_xattn_wv, L1_xattn_wo,
           L1_xattn_norm_w):
    import numpy as np
    import concourse.bacc as bacc
    from concourse.bass_utils import run_bass_kernel_spmd

    def by_partition(v):
        return np.asarray(v).reshape(2, P).T

    laid = {
        "x": x, "ctxT": np.asarray(ctx_1024).transpose(0, 2, 1),
        "WqT0": np.asarray(L0_xattn_Wq).T, "bq": np.asarray(L0_xattn_bq).reshape(4, 64).T,
        "WkT0": np.asarray(L0_xattn_Wk).T, "bk": by_partition(L0_xattn_bk),
        "WvT0": np.asarray(L0_xattn_Wv).T, "bv": np.asarray(L0_xattn_bv).reshape(4, 4, 16).transpose(1, 2, 0),
        "WoT0": np.asarray(L0_xattn_Wo).T, "bo": np.asarray(L0_xattn_bo).reshape(1, -1),
        "ln_g": by_partition(L0_xattn_ln_gamma), "ln_b": by_partition(L0_xattn_ln_beta),
        "wq1": L1_xattn_wq, "wk1": L1_xattn_wk, "wv1": L1_xattn_wv, "wo1": L1_xattn_wo,
        "norm_w": by_partition(L1_xattn_norm_w),
    }
    nc = bacc.Bacc("TRN2", target_bir_lowering=False, num_devices=1)
    arrays, args = {}, []
    for name, a in laid.items():
        a = np.ascontiguousarray(a)
        arrays[f"in_{name}"] = a
        args.append(nc.dram_tensor(f"in_{name}", a.shape, mybir.dt.from_np(a.dtype), kind="ExternalInput").ap())
    y = nc.dram_tensor("out_0", tuple(laid["x"].shape), F32, kind="ExternalOutput").ap()
    build(nc, *args, y)
    r = run_bass_kernel_spmd(nc, [arrays], core_ids=[0])
    return r.results[0]["out_0"]
```
